# Optimizing a Trainium2 kernel written in Bass

```python
import numpy as np
import jax
import jax.numpy as jnp

def _softmax(x, axis=-1):
    return jax.nn.softmax(x, axis=axis)

def _gelu(x):
    return jax.nn.gelu(x, approximate=True)

def _silu(x):
    return jax.nn.silu(x)

def _sigmoid(x):
    return jax.nn.sigmoid(x)

def _layernorm(x, axis=-1, eps=1e-05):
    m = jnp.mean(x, axis=axis, keepdims=True)
    v = jnp.var(x, axis=axis, keepdims=True)
    return (x - m) / jnp.sqrt(v + eps)

def _scatter_add(tgt, idx, src, axis=0):
    return tgt.at[idx].add(src)

def _segment_sum(src, seg, n):
    return jax.ops.segment_sum(src, seg, n)
kernel_name = 'mk_macaron_d1_jaxref_r8_287038'

def setup_inputs(seed: int=0):
    np.random.seed(seed)
    _w = jnp.asarray

    def _L0_attn_setup():
        import jax, jax.numpy as jnp
        import numpy as np
        N_HEADS = 1
        LATENT_DIM = 128
        SCALE = 1.0 / float(np.sqrt(LATENT_DIM * N_HEADS))
        key = jax.random.key(seed)
        kx, kq, ko = jax.random.split(key, 3)
        B, S, D = (4, 512, 128)
        x = jax.random.normal(kx, (B, S, D), dtype=jnp.float32)
        w_qkv = jax.random.normal(kq, (3 * N_HEADS * (LATENT_DIM // N_HEADS), D), dtype=jnp.float32) * 0.02
        w_o = jax.random.normal(ko, (LATENT_DIM, N_HEADS * (LATENT_DIM // N_HEADS)), dtype=jnp.float32) * 0.02
        return {'x': x, 'w_qkv': w_qkv, 'w_o': w_o}
    _L0_attn_in = _L0_attn_setup()

    def _L0_ffn_setup():
        import jax, jax.numpy as jnp
        import numpy as np
        DIM = 128
        DEPTH = 6
        HEADS = 16
        DIM_HEAD = 64
        WINDOW = 32
        INNER = HEADS * DIM_HEAD
        DIM_INNER = int(DIM * 4 * 2 / 3)
        QK_SCALE = 8.0

        def shift_tokens(t):
            a, s = jnp.split(t, 2, -1)
            s = jnp.pad(s, ((0, 0), (1, 0), (0, 0)))[:, :-1]
            return jnp.concatenate([a, s], -1)

        def l2norm(t):
            return t / jnp.maximum(jnp.linalg.norm(t, axis=-1, keepdims=True), 1e-12)

        def rotate_half(x):
            x1, x2 = jnp.split(x, 2, -1)
            return jnp.concatenate([-x2, x1], -1)

        def rotary_tables(n):
            half = jnp.arange(0, DIM_HEAD, 2, dtype=jnp.float32)
            inv_freq = 1.0 / 10000.0 ** (half / DIM_HEAD)
            t = jnp.arange(n, dtype=jnp.float32)
            freqs = t[:, None] * inv_freq[None, :]
            freqs = jnp.concatenate([freqs, freqs], -1)
            base_scale = (half + 0.4 * DIM_HEAD) / (1.4 * DIM_HEAD)
            power = (t - n // 2) / (WINDOW // 2)
            scale = base_scale[None, :] ** power[:, None]
            scale = jnp.concatenate([scale, scale], -1)
            return (freqs, scale)

        def local_attention(q, k, v):
            b, h, n, d = q.shape
            w = WINDOW
            nw = n // w
            bq = q.reshape(b, h, nw, w, d)
            bk = k.reshape(b, h, nw, w, d)
            bv = v.reshape(b, h, nw, w, d)

            def look(t):
                p = jnp.pad(t, ((0, 0), (0, 0), (1, 0), (0, 0), (0, 0)))
                return jnp.concatenate([p[:, :, :nw], p[:, :, 1:]], axis=3)
            bk2, bv2 = (look(bk), look(bv))
            seq = jnp.arange(n).reshape(nw, w)
            seq_p = jnp.pad(seq, ((1, 0), (0, 0)), constant_values=-1)
            jt = jnp.concatenate([seq_p[:nw], seq_p[1:]], axis=1)
            it = seq[:, :, None]
            jb = jt[:, None, :]
            mask = (it < jb) | (it > jb + w) | (jb == -1)
            sim = jnp.einsum('bhwie,bhwje->bhwij', bq, bk2) * QK_SCALE
            sim = jnp.where(mask, -jnp.finfo(sim.dtype).max, sim)
            attn = jax.nn.softmax(sim, -1)
            out = jnp.einsum('bhwij,bhwje->bhwie', attn, bv2)
            return out.reshape(b, h, n, d)

        def attn_layer(x, Wqkv, qs, ksc, Wo):
            b, n, _ = x.shape
            qkv = x @ Wqkv
            q, k, v = jnp.split(qkv, 3, -1)
            sh = lambda t: t.reshape(b, n, HEADS, DIM_HEAD).transpose(0, 2, 1, 3)
            q, k, v = (sh(q), sh(k), sh(v))
            q = l2norm(q) * qs
            k = l2norm(k) * ksc
            freqs, scale = rotary_tables(n)
            cos, sin = (jnp.cos(freqs), jnp.sin(freqs))
            q = q * cos * scale + rotate_half(q) * sin * scale
            inv = 1.0 / scale
            k = k * cos * inv + rotate_half(k) * sin * inv
            out = local_attention(q, k, v)
            out = out.transpose(0, 2, 1, 3).reshape(b, n, INNER)
            return out @ Wo

        def ffn_layer(x, g, bln, W1, b1, W2, b2):
            mu = x.mean(-1, keepdims=True)
            var = ((x - mu) ** 2).mean(-1, keepdims=True)
            xn = (x - mu) / jnp.sqrt(var + 1e-05) * g + bln
            hg = xn @ W1 + b1
            a, gate = jnp.split(hg, 2, -1)
            return a * jax.nn.gelu(gate, approximate=False) @ W2 + b2
        key = jax.random.key(seed)
        ks = jax.random.split(key, 8)
        B, N = (2, 256)
        init = lambda k, shape: jax.random.normal(k, shape, jnp.float32) * 0.02
        return {'x': jax.random.normal(ks[0], (B, N, DIM), jnp.float32), 'Wqkv': init(ks[1], (DEPTH, DIM, 3 * INNER)), 'q_scale': jnp.ones((DEPTH, DIM_HEAD), jnp.float32), 'k_scale': jnp.ones((DEPTH, DIM_HEAD), jnp.float32), 'Wo': init(ks[2], (DEPTH, INNER, DIM)), 'ln_g': jnp.ones((DEPTH, DIM), jnp.float32), 'ln_b': jnp.zeros((DEPTH, DIM), jnp.float32), 'W1': init(ks[3], (DEPTH, DIM, 2 * DIM_INNER)), 'b1': jnp.zeros((DEPTH, 2 * DIM_INNER), jnp.float32), 'W2': init(ks[4], (DEPTH, DIM_INNER, DIM)), 'b2': jnp.zeros((DEPTH, DIM), jnp.float32)}
    _L0_ffn_in = _L0_ffn_setup()
    _d = {'L0_attn_x': _L0_attn_in['x'], 'L0_attn_w_qkv': _L0_attn_in['w_qkv'], 'L0_attn_w_o': _L0_attn_in['w_o'], 'L0_ffn_Wqkv': _L0_ffn_in['Wqkv'], 'L0_ffn_q_scale': _L0_ffn_in['q_scale'], 'L0_ffn_k_scale': _L0_ffn_in['k_scale'], 'L0_ffn_Wo': _L0_ffn_in['Wo'], 'L0_ffn_ln_g': _L0_ffn_in['ln_g'], 'L0_ffn_ln_b': _L0_ffn_in['ln_b'], 'L0_ffn_W1': _L0_ffn_in['W1'], 'L0_ffn_b1': _L0_ffn_in['b1'], 'L0_ffn_W2': _L0_ffn_in['W2'], 'L0_ffn_b2': _L0_ffn_in['b2']}
    _x0 = _d['L0_attn_x']
    _d['L0_attn_x'] = jax.random.normal(jax.random.fold_in(jax.random.key(seed), 1), (4, 512, 128), dtype=_x0.dtype)
    del _x0
    return _d

def reference(L0_attn_x, L0_attn_w_qkv, L0_attn_w_o, L0_ffn_Wqkv, L0_ffn_q_scale, L0_ffn_k_scale, L0_ffn_Wo, L0_ffn_ln_g, L0_ffn_ln_b, L0_ffn_W1, L0_ffn_b1, L0_ffn_W2, L0_ffn_b2):

    def _L0_attn_ref(x, w_qkv, w_o):
        import jax, jax.numpy as jnp
        import numpy as np
        N_HEADS = 1
        LATENT_DIM = 128
        SCALE = 1.0 / float(np.sqrt(LATENT_DIM * N_HEADS))
        B, S, _ = x.shape
        qkv = jnp.einsum('bsd,fd->bsf', x, w_qkv)
        qkv = qkv.reshape(B, S, N_HEADS, 3 * LATENT_DIM).transpose(0, 2, 1, 3)
        q, k, v = jnp.split(qkv, 3, axis=-1)
        attn_logits = jnp.einsum('bhqd,bhkd->bhqk', q, k) * SCALE
        attention = jax.nn.softmax(attn_logits, axis=1)
        values = jnp.einsum('bhqk,bhkd->bhqd', attention, v)
        values = values.transpose(0, 2, 1, 3).reshape(B, S, N_HEADS * LATENT_DIM)
        return jnp.einsum('bsf,of->bso', values, w_o)

    def _L0_ffn_ref(x, Wqkv, q_scale, k_scale, Wo, ln_g, ln_b, W1, b1, W2, b2):
        import jax, jax.numpy as jnp
        import numpy as np
        DIM = 128
        DEPTH = 6
        HEADS = 16
        DIM_HEAD = 64
        WINDOW = 32
        INNER = HEADS * DIM_HEAD
        DIM_INNER = int(DIM * 4 * 2 / 3)
        QK_SCALE = 8.0

        def shift_tokens(t):
            a, s = jnp.split(t, 2, -1)
            s = jnp.pad(s, ((0, 0), (1, 0), (0, 0)))[:, :-1]
            return jnp.concatenate([a, s], -1)

        def l2norm(t):
            return t / jnp.maximum(jnp.linalg.norm(t, axis=-1, keepdims=True), 1e-12)

        def rotate_half(x):
            x1, x2 = jnp.split(x, 2, -1)
            return jnp.concatenate([-x2, x1], -1)

        def rotary_tables(n):
            half = jnp.arange(0, DIM_HEAD, 2, dtype=jnp.float32)
            inv_freq = 1.0 / 10000.0 ** (half / DIM_HEAD)
            t = jnp.arange(n, dtype=jnp.float32)
            freqs = t[:, None] * inv_freq[None, :]
            freqs = jnp.concatenate([freqs, freqs], -1)
            base_scale = (half + 0.4 * DIM_HEAD) / (1.4 * DIM_HEAD)
            power = (t - n // 2) / (WINDOW // 2)
            scale = base_scale[None, :] ** power[:, None]
            scale = jnp.concatenate([scale, scale], -1)
            return (freqs, scale)

        def local_attention(q, k, v):
            b, h, n, d = q.shape
            w = WINDOW
            nw = n // w
            bq = q.reshape(b, h, nw, w, d)
            bk = k.reshape(b, h, nw, w, d)
            bv = v.reshape(b, h, nw, w, d)

            def look(t):
                p = jnp.pad(t, ((0, 0), (0, 0), (1, 0), (0, 0), (0, 0)))
                return jnp.concatenate([p[:, :, :nw], p[:, :, 1:]], axis=3)
            bk2, bv2 = (look(bk), look(bv))
            seq = jnp.arange(n).reshape(nw, w)
            seq_p = jnp.pad(seq, ((1, 0), (0, 0)), constant_values=-1)
            jt = jnp.concatenate([seq_p[:nw], seq_p[1:]], axis=1)
            it = seq[:, :, None]
            jb = jt[:, None, :]
            mask = (it < jb) | (it > jb + w) | (jb == -1)
            sim = jnp.einsum('bhwie,bhwje->bhwij', bq, bk2) * QK_SCALE
            sim = jnp.where(mask, -jnp.finfo(sim.dtype).max, sim)
            attn = jax.nn.softmax(sim, -1)
            out = jnp.einsum('bhwij,bhwje->bhwie', attn, bv2)
            return out.reshape(b, h, n, d)

        def attn_layer(x, Wqkv, qs, ksc, Wo):
            b, n, _ = x.shape
            qkv = x @ Wqkv
            q, k, v = jnp.split(qkv, 3, -1)
            sh = lambda t: t.reshape(b, n, HEADS, DIM_HEAD).transpose(0, 2, 1, 3)
            q, k, v = (sh(q), sh(k), sh(v))
            q = l2norm(q) * qs
            k = l2norm(k) * ksc
            freqs, scale = rotary_tables(n)
            cos, sin = (jnp.cos(freqs), jnp.sin(freqs))
            q = q * cos * scale + rotate_half(q) * sin * scale
            inv = 1.0 / scale
            k = k * cos * inv + rotate_half(k) * sin * inv
            out = local_attention(q, k, v)
            out = out.transpose(0, 2, 1, 3).reshape(b, n, INNER)
            return out @ Wo

        def ffn_layer(x, g, bln, W1, b1, W2, b2):
            mu = x.mean(-1, keepdims=True)
            var = ((x - mu) ** 2).mean(-1, keepdims=True)
            xn = (x - mu) / jnp.sqrt(var + 1e-05) * g + bln
            hg = xn @ W1 + b1
            a, gate = jnp.split(hg, 2, -1)
            return a * jax.nn.gelu(gate, approximate=False) @ W2 + b2
        for i in range(DEPTH):
            x = attn_layer(shift_tokens(x), Wqkv[i], q_scale[i], k_scale[i], Wo[i]) + x
            x = ffn_layer(shift_tokens(x), ln_g[i], ln_b[i], W1[i], b1[i], W2[i], b2[i]) + x
        return x
    x = L0_attn_x
    x = x + 0.5 * _L0_ffn_ref(_layernorm(x, axis=-1), L0_ffn_Wqkv, L0_ffn_q_scale, L0_ffn_k_scale, L0_ffn_Wo, L0_ffn_ln_g, L0_ffn_ln_b, L0_ffn_W1, L0_ffn_b1, L0_ffn_W2, L0_ffn_b2)
    x = x + _L0_attn_ref(_layernorm(x, axis=-1), L0_attn_w_qkv, L0_attn_w_o)
    x = x + 0.5 * _L0_ffn_ref(_layernorm(x, axis=-1), L0_ffn_Wqkv, L0_ffn_q_scale, L0_ffn_k_scale, L0_ffn_Wo, L0_ffn_ln_g, L0_ffn_ln_b, L0_ffn_W1, L0_ffn_b1, L0_ffn_W2, L0_ffn_b2)
    return x

_drawn_inputs = setup_inputs


def setup_inputs(seed=0):
    import zlib

    import numpy as np

    out = dict(_drawn_inputs(seed))
    spreads = {'L0_ffn_q_scale': (1.0, 0.6),
     'L0_ffn_k_scale': (1.0, 0.6),
     'L0_ffn_ln_g': (1.0, 0.6),
     'L0_ffn_ln_b': (0.0, 0.8),
     'L0_ffn_b1': (0.0, 0.415),
     'L0_ffn_b2': (0.0, 0.1)}
    factors = {'L0_ffn_W1': 3.544}
    for name, (base, spread) in spreads.items():
        noise = np.random.default_rng([zlib.crc32(name.encode()), seed]).standard_normal(out[name].shape)
        drawn = base * np.exp(spread * noise) if base else spread * noise
        out[name] = jnp.asarray(drawn.astype(out[name].dtype))
    for name, factor in factors.items():
        out[name] = (out[name] * factor).astype(out[name].dtype)
    return out
```

```python
from contextlib import ExitStack

import concourse.bass as bass
import numpy as np
from concourse import mybir

F32 = mybir.dt.float32
BF16 = mybir.dt.bfloat16
ALU = mybir.AluOpType
ACT = mybir.ActivationFunctionType
AX_X = mybir.AxisListType.X

P = 128
SEQS, SEQ = 4, 512
TILES = SEQS * SEQ // P
TPS = SEQ // P
DEPTH = 6
HEADS, DH = 16, 64
INNER = HEADS * DH
HALF = INNER // 2
UH = HEADS // 2
PAIRS = UH // 2
WIN = 32
WPT = P // WIN
KEYS = 2 * WIN
HID = int(P * 4 * 2 / 3)
CHUNKS = [(c, min(P, HID - c)) for c in range(0, HID, P)]
NCH = len(CHUNKS)
SP1 = SEQ + 1
UNITS = 2 * TILES
QK_SCALE = 8.0
NORM_FLOOR = 1e-24
EPS = 1e-5
MASKED = -1e30
ONE, DMA_ONE = 1, 16
LN_PASS = 4 + 4 * DEPTH + 4


def rotary_base():
    half = np.arange(0, DH, 2, dtype=np.float32)
    inv_freq = (1.0 / np.float32(10000.0) ** (half / np.float32(DH))).astype(np.float32)
    t = np.arange(SEQ, dtype=np.float32)
    freqs = t[:, None] * inv_freq[None, :]
    freqs = np.concatenate([freqs, freqs], -1)
    base = (half + 0.4 * DH) / (1.4 * DH)
    power = (t - SEQ // 2) / (WIN // 2)
    scale = base[None, :].astype(np.float64) ** power[:, None]
    scale = np.concatenate([scale, scale], -1)
    cos, sin = np.cos(freqs.astype(np.float64)), np.sin(freqs.astype(np.float64))
    sign = np.where(np.arange(DH) < DH // 2, 1.0, -1.0)
    out = np.empty((2, 2, SEQ, DH))
    for qk, s in enumerate((scale, 1.0 / scale)):
        out[0, qk] = cos * s
        out[1, qk] = sin * s * sign
    out = out.reshape(2, 2, TPS, P, DH).transpose(3, 2, 0, 1, 4)
    return np.ascontiguousarray(out.astype(np.float32))


def score_mask():
    ws, hp, q, tile, g, key = np.meshgrid(
        np.arange(2), np.arange(2), np.arange(WIN), np.arange(TILES), np.arange(2), np.arange(KEYS), indexing="ij")
    prev = key < WIN
    seen = np.where(prev, key >= q, key - WIN <= q)
    first = (tile % TPS == 0) & (g == 0) & (ws == 0)
    seen &= ~(first & prev)
    return np.where(seen, 0.0, MASKED).reshape(P, TILES, 2 * KEYS)


def build(nc, x, w_qkv, w_o, Wqkv, Wo, W1, W2, scales_dram, vecs_dram, rot_dram, mask_dram, ident_dram, out):
    ctx = ExitStack()
    with ctx:
        def sb(name, shape, dt=F32):
            return ctx.enter_context(nc.sbuf_tensor(name, shape, dt))

        def sem(name):
            return ctx.enter_context(nc.semaphore(name))

        ident = sb("ident", [P, P])
        ident16 = sb("ident16", [P, P], BF16)
        mean_mat = sb("mean_mat", [P, P])
        minus_half = sb("minus_half", [P, UH * 2])
        mask = sb("mask", [P, TILES, 2 * KEYS], BF16)
        rot_base = sb("rot_base", [P, TPS * 2, 2, DH])
        rot = sb("rot", [P, TPS, 2, 2, DH])
        scales = sb("scales", [P, DEPTH, 2, DH])
        vecs = sb("vecs", [P, DEPTH, 3 + 2 * NCH])
        vec = sb("vec", [P, 3 + 2 * NCH])
        wqkv = sb("wqkv", [P, 3 * INNER])
        wo = sb("wo", [P, 2, PAIRS // 2, 2, P])
        w1 = sb("w1", [P, 2 * HID])
        w2 = sb("w2", [P, NCH, P])
        xtok = sb("xtok", [P, TILES, P])
        x0 = sb("x0", [P, SEQS, SEQ])
        xa = sb("xa", [P, SEQS, SP1])
        xb = sb("xb", [P, SEQS, SP1])
        xs = [sb(f"xs{h}", [P, P]) for h in range(2)]
        sq = sb("sq", [P, 2, UH, DH])
        rot_c = sb("rot_c", [P, 2, UH, DH])
        rot_s = sb("rot_s", [P, 2, UH, DH])
        rot_sum = sb("rot_sum", [P, 2, UH, DH])
        qkn = sb("qkn", [P, 2, UH, DH])
        ss = sb("ss", [P, 2 * UH])
        ssc = sb("ssc", [P, 2 * UH])
        rn = sb("rn", [P, 2 * UH])
        qbd = [sb(f"qbd{h}", [P, PAIRS, WPT, 2, WIN]) for h in range(2)]
        kt = [sb(f"kt{h}", [P, PAIRS, WIN + P]) for h in range(2)]
        vn = [sb(f"vn{h}", [P, HALF]) for h in range(2)]
        vs = [sb(f"vs{h}", [P, HALF]) for h in range(2)]
        vtail = [sb(f"vtail{h}", [P, HALF]) for h in range(2)]
        dif = [sb(f"dif{h}", [P, PAIRS * 2, KEYS]) for h in range(2)]
        prob = [sb(f"prob{h}", [P, PAIRS * 2, KEYS]) for h in range(2)]
        row_max = [sb(f"row_max{h}", [P, PAIRS * 2]) for h in range(2)]
        den = [sb(f"den{h}", [P, PAIRS * 2]) for h in range(2)]
        rden = [sb(f"rden{h}", [P, PAIRS, 2]) for h in range(2)]
        pt = [sb(f"pt{h}", [P, PAIRS, P]) for h in range(2)]
        on = [sb(f"on{h}", [P, 2, PAIRS, DH]) for h in range(2)]
        ot = [sb(f"ot{h}", [P, 2, PAIRS // 2, 2, 2, WIN]) for h in range(2)]
        fs = [sb(f"fs{s}", [P, SEQ]) for s in range(SEQS)]
        fd = [sb(f"fd{s}", [P, SEQ]) for s in range(SEQS)]
        fsq = [sb(f"fsq{s}", [P, SEQ]) for s in range(SEQS)]
        fn = [sb(f"fn{s}", [P, SEQ]) for s in range(SEQS)]
        var = sb("var", [P, SEQS, TPS])
        rstd = sb("rstd", [P, SEQS, TPS])
        gate = [sb(f"gate{i}", [P, SEQ]) for i in range(2)]
        hid = [sb(f"hid{i}", [P, SEQ]) for i in range(NCH)]
        wqkv_rows = sb("wqkv_rows", [P, P])
        wo_rows = sb("wo_rows", [P, P])
        wvT = sb("wvT", [P, P])
        woT = sb("woT", [P, P])
        hsum = sb("hsum", [P, SEQS])
        vsum = sb("vsum", [P, SEQS])

        ps = [ctx.enter_context(nc.psum_tensor(f"bank{i}", [P, 512], F32)) for i in range(3, 8)]
        qk_ps = ctx.enter_context(nc.psum_tensor("qk_ps", [P, 2, 512], F32))
        v_ps = ctx.enter_context(nc.psum_tensor("v_ps", [P, 512], F32))
        tr0, tr1, s_ps, o0_ps, o1_ps = ps
        banks = [qk_ps[:, 0, :], qk_ps[:, 1, :], v_ps[:, :], tr0[:, :], tr1[:, :], s_ps[:, :], o0_ps[:, :], o1_ps[:, :]]

        consts_in = sem("consts_in")
        consts_ready = sem("consts_ready")
        zeros_ready = sem("zeros_ready")
        vecs_in = sem("vecs_in")
        x_in = sem("x_in")
        wqkv_in = sem("wqkv_in")
        wo_in = sem("wo_in")
        w1_in = sem("w1_in")
        w2_in = sem("w2_in")
        mid_w_in = sem("mid_w_in")
        out_done = sem("out_done")
        rot_ready = sem("rot_ready")
        vec_ready = sem("vec_ready")
        xs_ready = sem("xs_ready")
        qk_ready = sem("qk_ready")
        v_ready = sem("v_ready")
        sq_ready = sem("sq_ready")
        rot_parts = sem("rot_parts")
        rot_added = sem("rot_added")
        ss_raw = sem("ss_raw")
        ss_ready = sem("ss_ready")
        rn_ready = sem("rn_ready")
        qkn_ready = sem("qkn_ready")
        qt_ready = sem("qt_ready")
        ktp_ready = sem("ktp_ready")
        qbd_ready = sem("qbd_ready")
        k_head = sem("k_head")
        kt_ready = sem("kt_ready")
        s_ready = sem("s_ready")
        max_ready = sem("max_ready")
        dif_ready = sem("dif_ready")
        prob_ready = sem("prob_ready")
        den_ready = sem("den_ready")
        rden_ready = sem("rden_ready")
        ptp_ready = sem("ptp_ready")
        pt_ready = sem("pt_ready")
        vn_ready = sem("vn_ready")
        vhead_ready = sem("vhead_ready")
        vs_in = [sem(f"vs_in{h}") for h in range(2)]
        vtail_in = [sem(f"vtail_in{h}") for h in range(2)]
        o_ready = sem("o_ready")
        on_ready = sem("on_ready")
        otp_ready = sem("otp_ready")
        ot_ready = sem("ot_ready")
        y_ready = sem("y_ready")
        y_added = sem("y_added")
        xa_ready = sem("xa_ready")
        x0_ready = sem("x0_ready")
        fs_ready = sem("fs_ready")
        mean_ready = sem("mean_ready")
        fd_ready = sem("fd_ready")
        fsq_ready = sem("fsq_ready")
        varp_ready = sem("varp_ready")
        var_ready = sem("var_ready")
        rstd_ready = sem("rstd_ready")
        rb_ready = sem("rb_ready")
        fn_raw = sem("fn_raw")
        fn_ready = sem("fn_ready")
        gated_ps = sem("gated_ps")
        gate_ready = sem("gate_ready")
        hid_ready = sem("hid_ready")
        fy_ready = sem("fy_ready")
        tx_ready = sem("tx_ready")
        tw_ready = sem("tw_ready")
        tw_out = sem("tw_out")
        hsum_ready = sem("hsum_ready")
        vsum_ps = sem("vsum_ps")
        vsum_ready = sem("vsum_ready")
        ymid_ps = sem("ymid_ps")


        def first_ln(p):
            return LN_PASS * p

        def over_units(eng, step):
            step(0, 0, True, True, False, False)
            step(0, 1, True, True, True, False)
            with eng.Fori(1, TILES - 1) as t:
                step(t, 0, True, True, True, True)
                step(t, 1, True, True, True, True)
            step(TILES - 1, 0, True, True, True, True)
            step(TILES - 1, 1, False, True, True, True)
            step(TILES, 0, False, False, True, True)
            step(TILES, 1, False, False, False, True)

        block = ctx.enter_context(nc.Block())

        @block.sync
        def _(sp):
            for released in (*vs_in, *vtail_in):
                sp.sem_inc(released, DMA_ONE)
            sp.dma_start(xtok[:, :, :], x.rearrange("(n p) d -> p n d", p=P)).then_inc(x_in, 16)
            sp.dma_start(ident[:, :], ident_dram).then_inc(consts_in, 16)
            sp.dma_start(rot_base[:, :, :, :], rot_dram).then_inc(consts_in, 16)
            sp.dma_start(mask[:, :, :], mask_dram).then_inc(consts_in, 16)
            sp.dma_start(scales[:, :, :, :], scales_dram.unsqueeze(0).to_broadcast([P, DEPTH, 2, DH])).then_inc(vecs_in, 16)
            sp.dma_start(vecs[:, :, :], vecs_dram).then_inc(vecs_in, 16)
            sp.dma_start(wqkv_rows[:, :], w_qkv[2 * P:3 * P, :]).then_inc(mid_w_in, 16)
            sp.dma_start(wo_rows[:, :], w_o).then_inc(mid_w_in, 16)

            def shift_values(U, TG, h):
                sp.wait_ge(vn_ready, U + 1 + ONE)
                sp.dma_start(vs[h][WIN:P, :], vn[h][0:P - WIN, :]).then_inc(vs_in[h], 16)
                sp.wait_ge(vhead_ready, U + 1)
                sp.dma_start(vtail[h][0:WIN, :], vn[h][P - WIN:P, :]).then_inc(vtail_in[h], 16)

            for p in range(2):
                with sp.Fori(0, DEPTH) as l:
                    g = l + p * DEPTH
                    sp.wait_ge(y_ready, g * UNITS + ONE)
                    sp.wait_ge(consts_ready, 1)
                    for part in range(3):
                        sp.dma_start(wqkv[:, part * INNER:(part + 1) * INNER],
                                     Wqkv[bass.ds(l, 1), :, part * INNER:(part + 1) * INNER]
                                     .rearrange("a p n -> p (a n)")).then_inc(wqkv_in, 16)
                    sp.dma_start(wo[:, :, :, :, :].rearrange("p c g b n -> p (c g b n)"),
                                 Wo[bass.ds(l, 1), :, :].rearrange("a p n -> p (a n)")).then_inc(wo_in, 16)
                    sp.wait_ge(fy_ready, g * SEQS + ONE)
                    sp.wait_ge(consts_ready, 1)
                    sp.dma_start(w1[:, :], W1[bass.ds(l, 1), :, :].rearrange("a p n -> p (a n)")).then_inc(w1_in, 16)
                    for j, (c, n) in enumerate(CHUNKS):
                        sp.dma_start(w2[0:n, j, :], W2[bass.ds(l, 1), c:c + n, :].rearrange("a p n -> p (a n)")
                                     ).then_inc(w2_in, 16)
                    with sp.Fori(0, TILES) as t:
                        for h in range(2):
                            shift_values(g * UNITS + 2 * t + h, g * TILES + t, h)
                        sp.wait_ge(consts_ready, 1)
            sp.wait_ge(tx_ready, 2 * SEQS)
            sp.wait_ge(x0_ready, 5 * SEQS)
            sp.dma_start(out.rearrange("(n p) d -> p n d", p=P), xtok[:, :, :]).then_inc(out_done, 16)
            sp.wait_ge(out_done, 16)

        @block.gpsimd
        def _(pool):
            for released in (rot_added, rn_ready):
                pool.sem_inc(released, ONE)
            for h in range(2):
                nc.gpsimd.memset(vtail[h][:, :], 0.0).then_inc(zeros_ready, 1)
                nc.gpsimd.memset(qbd[h][:, :, :, :, :], 0.0).then_inc(zeros_ready, 1)
                nc.gpsimd.memset(kt[h][:, :, :], 0.0).then_inc(zeros_ready, 1)
            nc.gpsimd.memset(mean_mat[:, :], 1.0 / P).then_inc(zeros_ready, 1)
            nc.gpsimd.memset(minus_half[:, :], -0.5).then_inc(zeros_ready, 1)
            nc.gpsimd.memset(xa[:, :, :], 0.0).then_inc(zeros_ready, 1)
            nc.gpsimd.memset(xb[:, :, :], 0.0).then_inc(zeros_ready, 1)
            pool.wait_ge(zeros_ready, 10)

            def inverse_std(n, s):
                pool.wait_ge(var_ready, n + 1)
                nc.gpsimd.tensor_tensor(rstd[:, s, :], var[:, s, :], minus_half[:, 0:TPS], ALU.pow).then_inc(rstd_ready, 1)

            def front(U):
                pool.wait_ge(rot_parts, U + 1 + ONE)
                pool.wait_ge(qkn_ready, U + ONE)
                nc.gpsimd.tensor_tensor(rot_sum[:, :, :, :], rot_c[:, :, :, :], rot_s[:, :, :, :], ALU.add
                                        ).then_inc(rot_added, 1)
                pool.wait_ge(ss_ready, U + 1)
                nc.gpsimd.tensor_tensor(rn[:, :], ssc[:, :], minus_half[:, :], ALU.pow).then_inc(rn_ready, 1)

            for p in range(2):
                for s in range(SEQS):
                    inverse_std(first_ln(p) + s, s)
                with pool.Fori(0, DEPTH) as l:
                    g = l + p * DEPTH
                    front(g * UNITS)

                    def step(t, h, fr, mid, back1, back2):
                        U = g * UNITS + 2 * t + h
                        if fr:
                            front(U + 1)

                    over_units(pool, step)
                    for s in range(SEQS):
                        inverse_std(first_ln(p) + SEQS + SEQS * l + s, s)
                if p == 0:
                    for s in range(SEQS):
                        inverse_std(first_ln(1) - SEQS + s, s)

        @block.scalar
        def _(act):
            for released in (vn_ready, qbd_ready, kt_ready, ot_ready):
                act.sem_inc(released, ONE)
            act.wait_ge(consts_in, 48)
            act.wait_ge(zeros_ready, 10)
            nc.scalar.activation(ident16[:, :], ident[:, :], ACT.Copy).then_inc(consts_ready, 1)
            for s in range(SEQS):
                act.wait_ge(tx_ready, s + 1)
                nc.scalar.activation(x0[:, s, :], banks[s], ACT.Copy).then_inc(x0_ready, 1)

            def ln_squares(n, s):
                act.wait_ge(fd_ready, n + 1)
                nc.scalar.activation(fsq[s][:, :], fd[s][:, :], ACT.Square).then_inc(fsq_ready, 1)

            def macaron_ln(n0):
                for s in range(SEQS):
                    ln_squares(n0 + s, s)

            def stage_xs(U, t, h, after):
                act.wait_ge(zeros_ready, 10)
                if after:
                    act.wait_ge(v_ready, U - 1)
                at = (t // TPS) * SP1 + (t % TPS) * P
                flat = xa[:, :, :].rearrange("p s n -> p (s n)")
                nc.scalar.activation(xs[h][0:DH, :], flat[0:DH, bass.ds(at + 1, P)], ACT.Copy)
                nc.scalar.activation(xs[h][DH:P, :], flat[DH:P, bass.ds(at, P)], ACT.Copy).then_inc(xs_ready, 1)

            def squares(U):
                act.wait_ge(qk_ready, U + 1)
                act.wait_ge(ss_raw, U + ONE)
                nc.scalar.activation(sq[:, :, :, :].rearrange("p a h d -> p (a h d)"),
                                     qk_ps[:, :, :].rearrange("p a n -> p (a n)"), ACT.Square).then_inc(sq_ready, 1)

            def values(U, TG, h):
                act.wait_ge(v_ready, U + 1)
                act.wait_ge(vs_in[h], TG * 16 + DMA_ONE)
                act.wait_ge(vtail_in[h], TG * 16 + DMA_ONE)
                nc.scalar.activation(vn[h][:, :], v_ps[:, :], ACT.Copy).then_inc(vn_ready, 1)

            def heads_major(U, h):
                act.wait_ge(qt_ready, U + 1)
                for hp in range(2):
                    rows = slice(hp * DH, (hp + 1) * DH)
                    last = nc.scalar.activation(
                        qbd[h][rows, :, :, hp, :].rearrange("p a w q -> p (a w) q"),
                        tr0[rows, :].rearrange("p (aw q) -> p aw q", q=WIN), ACT.Copy)
                last.then_inc(qbd_ready, 1)
                nc.scalar.activation(kt[h][:, :, 0:WIN], kt[h][:, :, P:P + WIN], ACT.Copy).then_inc(k_head, 1)
                act.wait_ge(ktp_ready, U + 1)
                act.wait_ge(k_head, U + 1)
                nc.scalar.activation(kt[h][:, :, WIN:WIN + P], tr1[:, :].rearrange("p (a n) -> p a n", a=PAIRS),
                                     ACT.Copy).then_inc(kt_ready, 1)

            def exps(U, h):
                act.wait_ge(dif_ready, U + 1 + ONE)
                nc.scalar.activation(prob[h][:, :, :], dif[h][:, :, :], ACT.Exp, scale=QK_SCALE).then_inc(prob_ready, 1)

            for p in range(2):
                macaron_ln(first_ln(p))
                with act.Fori(0, DEPTH) as l:
                    g = l + p * DEPTH
                    act.wait_ge(xa_ready, first_ln(p) + SEQS + SEQS * l)
                    stage_xs(g * UNITS, 0, 0, False)
                    stage_xs(g * UNITS + 1, 0, 1, False)
                    squares(g * UNITS)
                    values(g * UNITS, g * TILES, 0)

                    def step(t, h, fr, mid, back1, back2):
                        U = g * UNITS + 2 * t + h
                        if mid:
                            heads_major(U, h)
                        if back1:
                            act.wait_ge(ptp_ready, U)
                            nc.scalar.activation(pt[1 - h][:, :, :].rearrange("p a n -> p (a n)"), tr0[:, :],
                                                 ACT.Copy).then_inc(pt_ready, 1)
                        if fr and not (isinstance(t, int) and t == TILES - 1):
                            stage_xs(U + 2, t + 1, h, True)
                        if fr:
                            squares(U + 1)
                        if back2:
                            act.wait_ge(otp_ready, U - 1)
                            nc.scalar.activation(ot[h][:, :, :, :, :, :].rearrange("p a b c d q -> p (a b c d q)"),
                                                 tr1[:, :], ACT.Copy).then_inc(ot_ready, 1)
                        if mid:
                            exps(U, h)
                        if fr:
                            values(U + 1, g * TILES + t + h, 1 - h)

                    over_units(act, step)

                    n0 = first_ln(p) + SEQS + SEQS * l
                    flat = xb
                    for s in range(SEQS):
                        act.wait_ge(y_added, g * UNITS + UNITS // SEQS * (s + 1) + ONE)
                        nc.scalar.activation(fs[s][0:DH, :], xb[0:DH, s, 1:SP1], ACT.Copy)
                        nc.scalar.activation(fs[s][DH:P, :], xb[DH:P, s, 0:SEQ], ACT.Copy).then_inc(fs_ready, 1)
                    for s in range(SEQS):
                        ln_squares(n0 + s, s)
                    act.wait_ge(vec_ready, g + 1)
                    for s in range(SEQS):
                        act.wait_ge(fn_raw, g * SEQS + s + 1)
                        nc.scalar.activation(fn[s][:, :], fd[s][:, :], ACT.Identity, bias=vec[:, 1:2], scale=vec[:, 0:1]
                                             ).then_inc(fn_ready, 1)
                    for s in range(SEQS):
                        for j, (c, m) in enumerate(CHUNKS):
                            i = s * NCH + j
                            act.wait_ge(gated_ps, g * SEQS * NCH + i + 1)
                            if i >= 2:
                                act.wait_ge(hid_ready, g * SEQS * NCH + i - 1)
                            nc.scalar.activation(gate[i % 2][0:m, :], banks[2 * (i % 2) + 1][0:m, :], ACT.Gelu,
                                                 bias=vec[0:m, 3 + NCH + j:4 + NCH + j]).then_inc(gate_ready, 1)
                if p == 0:
                    macaron_ln(first_ln(1) - SEQS)
                    act.wait_ge(tw_ready, 1)
                    nc.scalar.activation(wvT[:, :], banks[0][:, 0:P], ACT.Copy)
                    nc.scalar.activation(woT[:, :], banks[0][:, P:2 * P], ACT.Copy).then_inc(tw_out, 1)
                    act.wait_ge(vsum_ps, 1)
                    nc.scalar.activation(vsum[:, :], banks[1][:, 0:SEQS], ACT.Copy).then_inc(vsum_ready, 1)
            for s in range(SEQS):
                act.wait_ge(tx_ready, SEQS + s + 1)
                nc.scalar.activation(xtok[:, s * TPS:(s + 1) * TPS, :].rearrange("p n d -> p (n d)"), banks[s],
                                     ACT.Copy).then_inc(x0_ready, 1)

        @block.vector
        def _(dve):
            for released in (qkn_ready, ss_raw, y_added, rot_parts, dif_ready, on_ready):
                dve.sem_inc(released, ONE)
            dve.wait_ge(vecs_in, 32)
            dve.wait_ge(consts_ready, 1)
            dve.wait_ge(zeros_ready, 10)

            def centre(n, s, src):
                dve.wait_ge(mean_ready, n + 1)
                nc.vector.tensor_tensor(fd[s][:, :], src, banks[s % 2], ALU.subtract).then_inc(fd_ready, 1)

            def ln_variance(n, s):
                dve.wait_ge(varp_ready, n + 1)
                nc.vector.tensor_scalar(var[:, s, :], banks[2 + s % 2][:, 0:TPS], EPS, None, ALU.add).then_inc(var_ready, 1)

            def macaron_ln(n0):
                for s in range(SEQS):
                    centre(n0 + s, s, x0[:, s, :])
                for s in range(SEQS):
                    ln_variance(n0 + s, s)
                for s in range(SEQS):
                    dve.wait_ge(rb_ready, n0 + s + 1)
                    nc.vector.tensor_tensor(xa[:, s, 1:SP1], fd[s][:, :], banks[4 + s % 2], ALU.mult).then_inc(xa_ready, 1)

            def rotate(U, t):
                dve.wait_ge(sq_ready, U + 1)
                dve.wait_ge(rot_added, U + ONE)
                tt = t % TPS
                src = qk_ps[:, :, :].rearrange("p a (h d) -> p a h d", d=DH)
                tab = rot[:, :, :, :, :].rearrange("p t c a d -> p (t c a d)")

                def part(c, lo, n):
                    v = tab[:, bass.ds(tt * (4 * DH) + c * 2 * DH, 2 * DH)].rearrange("p (a d) -> p a d", a=2)
                    return v[:, :, lo:lo + n].unsqueeze(2).to_broadcast([P, 2, UH, n])

                nc.vector.tensor_tensor(rot_c[:, :, :, :], src, part(0, 0, DH), ALU.mult)
                H2 = DH // 2
                for lo in (0, H2):
                    to = H2 - lo
                    last = nc.vector.tensor_tensor(rot_s[:, :, :, to:to + H2], src[:, :, :, lo:lo + H2],
                                                   part(1, lo, H2), ALU.mult)
                last.then_inc(rot_parts, 1)

            def square_sums(U):
                nc.vector.tensor_reduce(ss[:, :], sq[:, :, :, :].rearrange("p a h d -> p (a h) d"), AX_X, ALU.add
                                        ).then_inc(ss_raw, 1)
                dve.wait_ge(ss_raw, U + 1 + ONE)
                dve.wait_ge(rn_ready, U + ONE)
                nc.vector.tensor_scalar(ssc[:, :], ss[:, :], NORM_FLOOR, None, ALU.max).then_inc(ss_ready, 1)

            def normalise(U):
                dve.wait_ge(rot_added, U + 1 + ONE)
                dve.wait_ge(rn_ready, U + 1 + ONE)
                nc.vector.tensor_tensor(qkn[:, :, :, :].rearrange("p a h d -> p (a h) d"),
                                        rot_sum[:, :, :, :].rearrange("p a h d -> p (a h) d"),
                                        rn[:, :].unsqueeze(2).to_broadcast([P, 2 * UH, DH]), ALU.mult
                                        ).then_inc(qkn_ready, 1)

            def softmax_front(U, h):
                dve.wait_ge(s_ready, U + 1)
                sc = s_ps[:, :].rearrange("p (a k) -> p a k", k=KEYS)
                nc.vector.tensor_reduce(row_max[h][:, :], sc, AX_X, ALU.max).then_inc(max_ready, 1)
                dve.wait_ge(max_ready, U + 1)
                nc.vector.tensor_tensor(dif[h][:, :, :], sc, row_max[h][:, :].unsqueeze(2)
                                        .to_broadcast([P, 2 * PAIRS, KEYS]), ALU.subtract).then_inc(dif_ready, 1)

            def softmax_sum(U, h):
                dve.wait_ge(prob_ready, U + 1)
                nc.vector.tensor_reduce(den[h][:, :], prob[h][:, :, :], AX_X, ALU.add).then_inc(den_ready, 1)
                dve.wait_ge(den_ready, U + 1)
                nc.vector.reciprocal(rden[h][:, :, :].rearrange("p a g -> p (a g)"), den[h][:, :]).then_inc(rden_ready, 1)

            def output_norm(U, h):
                dve.wait_ge(o_ready, U + 1)
                dve.wait_ge(rden_ready, U + 1)
                for gg, o in enumerate((o0_ps, o1_ps)):
                    last = nc.vector.tensor_tensor(
                        on[h][:, gg, :, :], o[:, 0:PAIRS * DH].rearrange("p (a d) -> p a d", d=DH),
                        rden[h][:, :, gg:gg + 1].to_broadcast([P, PAIRS, DH]), ALU.mult)
                last.then_inc(on_ready, 1)

            def value_head(U, TG, h, after):
                if after:
                    dve.wait_ge(o_ready, U - 1)
                dve.wait_ge(vtail_in[h], TG * 16 + DMA_ONE)
                nc.vector.tensor_copy(vs[h][0:WIN, :], vtail[h][0:WIN, :]).then_inc(vhead_ready, 1)

            def add_output(U, t, h):
                dve.wait_ge(y_ready, U + 1 + ONE)
                dve.wait_ge(y_added, U + ONE)
                at = (t // TPS) * SP1 + (t % TPS) * P + 1
                base = (xb if h else xa)[:, :, :].rearrange("p s n -> p (s n)")
                to = xb[:, :, :].rearrange("p s n -> p (s n)")
                nc.vector.tensor_tensor(to[:, bass.ds(at, P)], v_ps[:, 0:P], base[:, bass.ds(at, P)], ALU.add
                                        ).then_inc(y_added, 1)

            for p in range(2):
                if p == 0:
                    dve.wait_ge(x0_ready, SEQS)
                macaron_ln(first_ln(p))
                with dve.Fori(0, DEPTH) as l:
                    g = l + p * DEPTH
                    dve.wait_ge(xa_ready, first_ln(p) + SEQS + SEQS * l)
                    sc = scales[:, :, :, :].rearrange("p l a d -> p (l a d)")[:, bass.ds(l * (2 * DH), 2 * DH)]
                    nc.vector.tensor_tensor(rot[:, :, :, :, :].rearrange("p t c a d -> p (t c) (a d)"),
                                            rot_base[:, :, :, :].rearrange("p t a d -> p t (a d)"),
                                            sc.unsqueeze(1).to_broadcast([P, 2 * TPS, 2 * DH]), ALU.mult
                                            ).then_inc(rot_ready, 1)
                    NV = 3 + 2 * NCH
                    nc.vector.tensor_copy(vec[:, :], vecs[:, :, :].rearrange("p l v -> p (l v)")[:, bass.ds(l * NV, NV)]
                                          ).then_inc(vec_ready, 1)
                    dve.wait_ge(rot_ready, g + 1)
                    rotate(g * UNITS, 0)
                    square_sums(g * UNITS)
                    value_head(g * UNITS, g * TILES, 0, False)
                    normalise(g * UNITS)

                    def step(t, h, fr, mid, back1, back2):
                        U = g * UNITS + 2 * t + h
                        if fr:
                            rotate(U + 1, t + h)
                        if fr:
                            square_sums(U + 1)
                        if mid:
                            softmax_front(U, h)
                        if back2:
                            add_output(U - 2, t - 1, h)
                        if mid:
                            softmax_sum(U, h)
                        if back1:
                            output_norm(U - 1, 1 - h)
                        if fr:
                            value_head(U + 1, g * TILES + t + h, 1 - h, back1)
                            normalise(U + 1)

                    over_units(dve, step)

                    n0 = first_ln(p) + SEQS + SEQS * l
                    for s in range(SEQS):
                        centre(n0 + s, s, fs[s][:, :])
                    for s in range(SEQS):
                        ln_variance(n0 + s, s)
                    for s in range(SEQS):
                        dve.wait_ge(rb_ready, n0 + s + 1)
                        dve.wait_ge(fsq_ready, n0 + s + 1)
                        nc.vector.tensor_tensor(fd[s][:, :], fd[s][:, :], banks[4 + s % 2], ALU.mult).then_inc(fn_raw, 1)
                    for s in range(SEQS):
                        for j, (c, m) in enumerate(CHUNKS):
                            i = s * NCH + j
                            dve.wait_ge(gate_ready, g * SEQS * NCH + i + 1)
                            nc.vector.scalar_tensor_tensor(
                                hid[j][0:m, :], banks[2 * (i % 2)][0:m, :], vec[0:m, 3 + j:4 + j], gate[i % 2][0:m, :],
                                ALU.add, ALU.mult).then_inc(hid_ready, 1)
                        dve.wait_ge(fy_ready, g * SEQS + s + 1 + ONE)
                        nc.vector.scalar_tensor_tensor(
                            xa[:, s, 1:SP1], banks[6 + s % 2], vec[:, 2:3], xb[:, s, 1:SP1], ALU.add, ALU.add
                        ).then_inc(xa_ready, 1)
                dve.wait_ge(xa_ready, first_ln(p) + SEQS + SEQS * DEPTH)
                for s in range(SEQS):
                    nc.vector.scalar_tensor_tensor(x0[:, s, :], xa[:, s, 1:SP1], 0.5, x0[:, s, :], ALU.mult, ALU.add
                                                   ).then_inc(x0_ready, 1)
                if p == 0:
                    dve.wait_ge(x0_ready, 2 * SEQS)
                    macaron_ln(first_ln(1) - SEQS)
                    dve.wait_ge(xa_ready, first_ln(1))
                    nc.vector.tensor_reduce(hsum[:, :], xa[:, :, 1:SP1], AX_X, ALU.add).then_inc(hsum_ready, 1)
                    dve.wait_ge(ymid_ps, 1)
                    nc.vector.tensor_tensor(x0[:, :, :], x0[:, :, :],
                                            banks[2][:, 0:SEQS].unsqueeze(2).to_broadcast([P, SEQS, SEQ]), ALU.add
                                            ).then_inc(x0_ready, SEQS)
                    dve.wait_ge(x0_ready, 3 * SEQS)

        @block.tensor
        def _(pe):
            for released in (y_ready, fy_ready):
                pe.sem_inc(released, ONE)
            pe.wait_ge(consts_in, 48)
            pe.wait_ge(x_in, 16)
            pe.wait_ge(mid_w_in, 32)
            for s in range(SEQS):
                for j in range(TPS):
                    last = nc.tensor.transpose(banks[s][:, j * P:(j + 1) * P], xtok[:, s * TPS + j, :], ident[:, :])
                last.then_inc(tx_ready, 1)

            def ln_mean(n, s, src):
                if s >= 2:
                    pe.wait_ge(fd_ready, n - 1)
                nc.tensor.matmul(banks[s % 2], mean_mat[:, :], src, start=True, stop=True).then_inc(mean_ready, 1)

            def ln_var(n, s):
                pe.wait_ge(fsq_ready, n + 1)
                if s >= 2:
                    pe.wait_ge(var_ready, n - 1)
                for c in range(TPS):
                    last = nc.tensor.matmul(banks[2 + s % 2][:, c:c + 1], fsq[s][:, c * P:(c + 1) * P],
                                            mean_mat[:, 0:1], start=True, stop=True)
                last.then_inc(varp_ready, 1)

            def ln_spread(n, s, used, k):
                pe.wait_ge(rstd_ready, n + 1)
                if s >= 2:
                    pe.wait_ge(used, k - 1)
                for c in range(TPS):
                    last = nc.tensor.matmul(banks[4 + s % 2][:, c * P:(c + 1) * P],
                                            rstd[:, s, c:c + 1].to_broadcast([P, P]), ident[:, :], start=True, stop=True)
                last.then_inc(rb_ready, 1)

            def macaron_ln(n0):
                for s in range(SEQS):
                    ln_mean(n0 + s, s, x0[:, s, :])
                for s in range(SEQS):
                    ln_var(n0 + s, s)
                for s in range(SEQS):
                    ln_spread(n0 + s, s, xa_ready, n0 + s)

            def project(U, h, part):
                dst = (qk_ps[:, 0, :], qk_ps[:, 1, :], v_ps[:, :])[part]
                return nc.tensor.matmul(dst, xs[h][:, :], wqkv[:, part * INNER + h * HALF:part * INNER + (h + 1) * HALF],
                                        start=True, stop=True)

            def project_q(U, h):
                pe.wait_ge(xs_ready, U + 1)
                pe.wait_ge(rot_parts, U + ONE)
                project(U, h, 0)

            def project_k(U, h):
                project(U, h, 1).then_inc(qk_ready, 1)

            def project_v(U, h, Y):
                pe.wait_ge(vn_ready, U + ONE)
                if Y is not None:
                    pe.wait_ge(y_added, Y + 1 + ONE)
                project(U, h, 2).then_inc(v_ready, 1)

            def heads_major(U, t, h):
                pe.wait_ge(qkn_ready, U + 1 + ONE)
                pe.wait_ge(qbd_ready, U + ONE)
                if not (isinstance(t, int) and t == 0):
                    pe.wait_ge(pt_ready, U - 1)
                for a in range(PAIRS):
                    last = nc.tensor.transpose(tr0[:, a * P:(a + 1) * P],
                                               qkn[:, 0, 2 * a:2 * a + 2, :].rearrange("p h d -> p (h d)"), ident[:, :])
                last.then_inc(qt_ready, 1)
                pe.wait_ge(kt_ready, U + ONE)
                if not (isinstance(t, int) and t == 0):
                    pe.wait_ge(ot_ready, U - 2 + ONE)
                for a in range(PAIRS):
                    last = nc.tensor.transpose(tr1[:, a * P:(a + 1) * P],
                                               qkn[:, 1, 2 * a:2 * a + 2, :].rearrange("p h d -> p (h d)"), ident[:, :])
                last.then_inc(ktp_ready, 1)

            def scores(U, t, h):
                pe.wait_ge(qbd_ready, U + 1 + ONE)
                pe.wait_ge(kt_ready, U + 1 + ONE)
                pe.wait_ge(dif_ready, U + ONE)
                pe.wait_ge(consts_ready, 1)
                m = mask[:, :, :].rearrange("p t k -> p (t k)")[:, bass.ds(t * (2 * KEYS), 2 * KEYS)]
                nc.tensor.matmul(s_ps[:, :], ident16[:, :], m.unsqueeze(1).to_broadcast([P, PAIRS, 2 * KEYS]),
                                 start=True, stop=False, skip_group_check=True)
                for a in range(PAIRS):
                    for gg in range(2):
                        for ws in range(2):
                            w = 2 * gg + ws
                            last = nc.tensor.matmul(
                                s_ps[ws * 64:(ws + 1) * 64, (2 * a + gg) * KEYS:(2 * a + gg + 1) * KEYS],
                                qbd[h][:, a, w, :, :].rearrange("p b q -> p (b q)"),
                                kt[h][:, a, w * WIN:w * WIN + KEYS], start=False, stop=True, skip_group_check=True)
                last.then_inc(s_ready, 1)

            def prob_major(U, h, mid):
                pe.wait_ge(prob_ready, U + 1)
                if mid:
                    pe.wait_ge(qbd_ready, U + 2 + ONE)
                else:
                    pe.wait_ge(pt_ready, U)
                for a in range(PAIRS):
                    last = nc.tensor.transpose(tr0[:, a * P:(a + 1) * P],
                                               prob[h][:, 2 * a:2 * a + 2, :].rearrange("p g k -> p (g k)"), ident[:, :])
                last.then_inc(ptp_ready, 1)

            def out_major(U, h, mid):
                pe.wait_ge(on_ready, U + 1 + ONE)
                if mid:
                    pe.wait_ge(kt_ready, U + 3 + ONE)
                else:
                    pe.wait_ge(ot_ready, U + ONE)
                for gg in range(2):
                    for pg in range(PAIRS // 2):
                        c = gg * (PAIRS // 2) + pg
                        last = nc.tensor.transpose(tr1[:, c * P:(c + 1) * P],
                                                   on[h][:, gg, 2 * pg:2 * pg + 2, :].rearrange("p a d -> p (a d)"),
                                                   ident[:, :])
                last.then_inc(otp_ready, 1)

            def wait_to_weigh(U, TG, h):
                pe.wait_ge(pt_ready, U + 1)
                pe.wait_ge(vs_in[h], TG * 16 + 16 + DMA_ONE)
                pe.wait_ge(vhead_ready, U + 1)
                pe.wait_ge(on_ready, U + ONE)
                pe.wait_ge(vn_ready, U + 1 + ONE)

            def weigh_values(h):
                for gg in range(2):
                    rows = slice(gg * KEYS, (gg + 1) * KEYS)
                    o = (o0_ps, o1_ps)[gg]
                    for a in range(PAIRS):
                        for ws in range(2):
                            for hp in range(2):
                                c = 2 * ws + hp
                                last = nc.tensor.matmul(
                                    o[c * WIN:(c + 1) * WIN, a * DH:(a + 1) * DH],
                                    pt[h][rows, a, c * WIN:(c + 1) * WIN],
                                    (vn if ws else vs)[h][rows, (2 * a + hp) * DH:(2 * a + hp + 1) * DH],
                                    start=True, stop=True, skip_group_check=True)
                last.then_inc(o_ready, 1)

            def project_out(U, h, last_v):
                pe.wait_ge(ot_ready, U + 1 + ONE)
                pe.wait_ge(vn_ready, last_v + ONE)
                pe.wait_ge(y_added, U + ONE)
                n = 0
                for pg in range(PAIRS // 2):
                    for hp in range(2):
                        last = nc.tensor.matmul(v_ps[:, 0:P], wo[:, h, pg, hp, :], ot[h][:, :, pg, :, hp, :],
                                                start=n == 0, stop=n == PAIRS - 1)
                        n += 1
                last.then_inc(y_ready, 1)

            for p in range(2):
                pe.wait_ge(x0_ready, SEQS if p == 0 else 3 * SEQS)
                pe.wait_ge(zeros_ready, 10)
                macaron_ln(first_ln(p))
                with pe.Fori(0, DEPTH) as l:
                    g = l + p * DEPTH
                    pe.wait_ge(xa_ready, first_ln(p) + SEQS + SEQS * l)
                    pe.wait_ge(wqkv_in, 48 * g + 48)
                    pe.wait_ge(wo_in, 16 * g + 16)
                    project_q(g * UNITS, 0)
                    project_k(g * UNITS, 0)
                    project_v(g * UNITS, 0, None)

                    def step(t, h, fr, mid, back1, back2):
                        U = g * UNITS + 2 * t + h
                        if mid:
                            heads_major(U, t, h)
                        if fr:
                            project_q(U + 1, 1 - h)
                        if back1:
                            prob_major(U - 1, 1 - h, mid)
                        if fr:
                            project_k(U + 1, 1 - h)
                        if back2:
                            out_major(U - 2, h, mid)
                        if back1 and not back2:
                            wait_to_weigh(U - 1, g * TILES + t - 1 + h, 1 - h)
                        if mid:
                            scores(U, t, h)
                        if back1 and back2:
                            wait_to_weigh(U - 1, g * TILES + t - 1 + h, 1 - h)
                        if back2:
                            project_out(U - 2, h, U + 1 if mid else (g + 1) * UNITS)
                        if back1:
                            weigh_values(1 - h)
                        if fr:
                            project_v(U + 1, 1 - h, U - 2 if back2 else None)

                    over_units(pe, step)

                    n0 = first_ln(p) + SEQS + SEQS * l
                    pe.wait_ge(y_added, g * UNITS + UNITS + ONE)
                    for s in range(SEQS):
                        pe.wait_ge(fs_ready, g * SEQS + s + 1)
                        ln_mean(n0 + s, s, fs[s][:, :])
                    for s in range(SEQS):
                        ln_var(n0 + s, s)
                    for s in range(SEQS):
                        ln_spread(n0 + s, s, fn_raw, g * SEQS + s)
                    pe.wait_ge(w1_in, 16 * g + 16)
                    pe.wait_ge(w2_in, 16 * NCH * g + 16 * NCH)

                    def down(s):
                        for j, (c, m) in enumerate(CHUNKS):
                            pe.wait_ge(hid_ready, g * SEQS * NCH + s * NCH + j + 1)
                            if j == 0 and s >= 2:
                                pe.wait_ge(xa_ready, n0 + s - 1)
                            last = nc.tensor.matmul(banks[6 + s % 2], w2[0:m, j, :], hid[j][0:m, :],
                                                    start=j == 0, stop=j == NCH - 1)
                        last.then_inc(fy_ready, 1)

                    for s in range(SEQS):
                        pe.wait_ge(fn_ready, g * SEQS + s + 1)
                        for j, (c, m) in enumerate(CHUNKS):
                            i = s * NCH + j
                            if i >= 2:
                                pe.wait_ge(hid_ready, g * SEQS * NCH + i - 1)
                            for part in range(2):
                                last = nc.tensor.matmul(banks[2 * (i % 2) + part][0:m, :],
                                                        w1[:, part * HID + c:part * HID + c + m], fn[s][:, :],
                                                        start=True, stop=True)
                            last.then_inc(gated_ps, 1)
                        down(s)
                pe.wait_ge(x0_ready, 2 * SEQS if p == 0 else 4 * SEQS)
                if p == 0:
                    macaron_ln(first_ln(1) - SEQS)
                    pe.wait_ge(xa_ready, first_ln(1))
                    nc.tensor.transpose(banks[0][:, 0:P], wqkv_rows[:, :], ident[:, :])
                    nc.tensor.transpose(banks[0][:, P:2 * P], wo_rows[:, :], ident[:, :]).then_inc(tw_ready, 1)
                    pe.wait_ge(tw_out, 1)
                    pe.wait_ge(hsum_ready, 1)
                    nc.tensor.matmul(banks[1][:, 0:SEQS], wvT[:, :], hsum[:, :], start=True, stop=True).then_inc(vsum_ps, 1)
                    pe.wait_ge(vsum_ready, 1)
                    nc.tensor.matmul(banks[2][:, 0:SEQS], woT[:, :], vsum[:, :], start=True, stop=True).then_inc(ymid_ps, 1)
            for s in range(SEQS):
                for j in range(TPS):
                    last = nc.tensor.transpose(banks[s][:, j * P:(j + 1) * P], x0[:, s, j * P:(j + 1) * P], ident[:, :])
                last.then_inc(tx_ready, 1)


def layer_vectors(ln_g, ln_b, b1, b2):
    out = np.zeros((P, DEPTH, 3 + 2 * NCH), np.float32)
    for i, v in enumerate((ln_g, ln_b, b2)):
        out[:, :, i] = v.T
    for part in range(2):
        for j, (c, n) in enumerate(CHUNKS):
            out[0:n, :, 3 + part * NCH + j] = b1[:, part * HID + c:part * HID + c + n].T
    return out


def wo_rows_by_pair(w):
    return w.reshape(DEPTH, HEADS // 4, 2, 2, DH, P).transpose(0, 2, 4, 1, 3, 5).reshape(DEPTH, P, -1)


def kernel(**inputs):
    import ml_dtypes
    from concourse import bacc
    from concourse.bass_utils import run_bass_kernel_spmd

    given = {name.removeprefix("L0_"): np.asarray(a) for name, a in inputs.items()}
    x = given["attn_x"]
    nc = bacc.Bacc("TRN2", target_bir_lowering=False, num_devices=1)
    arrays = {
        "x_dram": x.reshape(-1, P),
        "w_qkv_dram": given["attn_w_qkv"],
        "w_o_dram": given["attn_w_o"],
        "layer_wqkv_dram": given["ffn_Wqkv"],
        "layer_wo_dram": wo_rows_by_pair(given["ffn_Wo"]),
        "layer_w1_dram": given["ffn_W1"],
        "layer_w2_dram": given["ffn_W2"],
        "layer_scales_dram": np.stack([given["ffn_q_scale"], given["ffn_k_scale"]], 1),
        "layer_vectors_dram": layer_vectors(*(given["ffn_" + n] for n in ("ln_g", "ln_b", "b1", "b2"))),
        "rotary_base_dram": rotary_base().reshape(P, TPS * 2, 2, DH),
        "score_mask_dram": score_mask().astype(ml_dtypes.bfloat16),
        "identity_dram": np.eye(P, dtype=np.float32),
    }
    arrays = {name: np.ascontiguousarray(a) for name, a in arrays.items()}
    args = [nc.dram_tensor(name, a.shape, mybir.dt.from_np(a.dtype), kind="ExternalInput").ap()
            for name, a in arrays.items()]
    out = nc.dram_tensor("out", (SEQS * SEQ, P), F32, kind="ExternalOutput").ap()
    build(nc, *args, out)
    r = run_bass_kernel_spmd(nc, [arrays], core_ids=[0])
    return r.results[0]["out"].reshape(x.shape)
```

```python
from contextlib import ExitStack

import concourse.bass as bass
import numpy as np
from concourse import mybir

F32 = mybir.dt.float32
BF16 = mybir.dt.bfloat16
F32R = mybir.dt.float32r
ALU = mybir.AluOpType
ACT = mybir.ActivationFunctionType
AX_X = mybir.AxisListType.X

P = 128
SEQS, SEQ = 4, 512
TILES = SEQS * SEQ // P
TPS = SEQ // P
DEPTH = 6
HEADS, DH = 16, 64
INNER = HEADS * DH
HALF = INNER // 2
UH = HEADS // 2
PAIRS = UH // 2
WIN = 32
WPT = P // WIN
KEYS = 2 * WIN
HID = int(P * 4 * 2 / 3)
CHUNKS = [(c, min(P, HID - c)) for c in range(0, HID, P)]
NCH = len(CHUNKS)
SP1 = SEQ + 1
UNITS = 2 * TILES
QK_SCALE = 8.0
DV = DH + 1
NORM_FLOOR = 1e-24
EPS = 1e-5
MASKED = -1e30
ONE, DMA_ONE = 1, 16
TWO = 2
LN_PASS = 4 + 4 * DEPTH + 4


def rotary_base():
    half = np.arange(0, DH, 2, dtype=np.float32)
    inv_freq = (1.0 / np.float32(10000.0) ** (half / np.float32(DH))).astype(np.float32)
    t = np.arange(SEQ, dtype=np.float32)
    freqs = t[:, None] * inv_freq[None, :]
    freqs = np.concatenate([freqs, freqs], -1)
    base = (half + 0.4 * DH) / (1.4 * DH)
    power = (t - SEQ // 2) / (WIN // 2)
    scale = base[None, :].astype(np.float64) ** power[:, None]
    scale = np.concatenate([scale, scale], -1)
    cos, sin = np.cos(freqs.astype(np.float64)), np.sin(freqs.astype(np.float64))
    sign = np.where(np.arange(DH) < DH // 2, 1.0, -1.0)
    out = np.empty((2, 2, SEQ, DH))
    for qk, s in enumerate((scale, 1.0 / scale)):
        out[0, qk] = cos * s
        out[1, qk] = sin * s * sign
    out = out.reshape(2, 2, TPS, P, DH).transpose(3, 2, 0, 1, 4)
    return np.ascontiguousarray(out.astype(np.float32))


def score_mask():
    ws, hp, q, tile, g, key = np.meshgrid(
        np.arange(2), np.arange(2), np.arange(WIN), np.arange(TILES), np.arange(2), np.arange(KEYS), indexing="ij")
    prev = key < WIN
    seen = np.where(prev, key >= q, key - WIN <= q)
    first = (tile % TPS == 0) & (g == 0) & (ws == 0)
    seen &= ~(first & prev)
    return np.where(seen, 0.0, MASKED).reshape(P, TILES, 2 * KEYS)


def build(nc, x, w_qkv, w_o, Wqkv, Wo, W1, W2, scales_dram, vecs_dram, rot_dram, mask_dram, ident_dram, out):
    ctx = ExitStack()
    with ctx:
        def sb(name, shape, dt=F32):
            return ctx.enter_context(nc.sbuf_tensor(name, shape, dt))

        def sem(name):
            return ctx.enter_context(nc.semaphore(name))

        ident = sb("ident", [P, P])
        ident16 = sb("ident16", [P, P], BF16)
        mean_mat = sb("mean_mat", [P, P])
        one = sb("one", [P, 1])
        minus_half = sb("minus_half", [P, UH * 2])
        mask = sb("mask", [P, TILES, 2 * KEYS], BF16)
        rot_base = sb("rot_base", [P, TPS * 2, 2, DH])
        rot = sb("rot", [P, TPS, 2, 2, DH])
        scales = sb("scales", [P, DEPTH, 2, DH])
        vecs = sb("vecs", [P, DEPTH, 3 + 2 * NCH])
        vec = sb("vec", [P, 3 + 2 * NCH])
        wqkv = sb("wqkv", [P, 3 * INNER])
        wqkv_hi = sb("wqkv_hi", [P, 3 * INNER], F32R)
        wqkv_lo = sb("wqkv_lo", [P, 3 * INNER], F32R)
        wo = sb("wo", [P, 2, PAIRS // 2, 2, P])
        w1 = sb("w1", [P, 2 * HID])
        w2 = sb("w2", [P, NCH, P])
        xtok = sb("xtok", [P, TILES, P])
        x0 = sb("x0", [P, SEQS, SEQ])
        xa = sb("xa", [P, SEQS, SP1])
        xb = sb("xb", [P, SEQS, SP1])
        xs_qk = sb("xs_qk", [P, P])
        xs_v = sb("xs_v", [P, P])
        xs_qk_hi, xs_qk_lo, xs_v_hi, xs_v_lo = (sb(n, [P, P], F32R) for n in ("xs_qk_hi", "xs_qk_lo", "xs_v_hi", "xs_v_lo"))
        sq = sb("sq", [P, 2, UH, DH])
        rot_c, rot_s, rot_sum = ([sb(f"{n}{h}", [P, 2, UH, DH]) for h in range(2)] for n in ("rot_c", "rot_s", "rot_sum"))
        qkn = [sb(f"qkn{h}", [P, 2, UH, DH]) for h in range(2)]
        ss = sb("ss", [P, 2 * UH])
        ssc = [sb(f"ssc{h}", [P, 2 * UH]) for h in range(2)]
        rn = [sb(f"rn{h}", [P, 2 * UH]) for h in range(2)]
        qbd = [sb(f"qbd{h}", [P, PAIRS, WPT, 2, WIN]) for h in range(2)]
        kt = [sb(f"kt{h}", [P, PAIRS, WIN + P]) for h in range(2)]
        vn = [sb(f"vn{h}", [P, UH, DV]) for h in range(2)]
        vs = [sb(f"vs{h}", [P, UH, DV]) for h in range(2)]
        vtail = [sb(f"vtail{h}", [P, UH, DV]) for h in range(2)]
        dif = [sb(f"dif{h}", [P, PAIRS * 2, KEYS]) for h in range(2)]
        prob = [sb(f"prob{h}", [P, PAIRS * 2, KEYS]) for h in range(2)]
        row_max = [sb(f"row_max{h}", [P, PAIRS * 2]) for h in range(2)]
        rden = sb("rden", [P, 2, PAIRS])
        pt = [sb(f"pt{h}", [P, PAIRS, P]) for h in range(2)]
        on = [sb(f"on{h}", [P, 2, PAIRS, DH]) for h in range(2)]
        ot = [sb(f"ot{h}", [P, 2, PAIRS // 2, 2, 2, WIN]) for h in range(2)]
        def by_sequence(pair):
            return [pair[s // 2][:, s % 2, :, :].rearrange("p h d -> p (h d)") for s in range(SEQS)]

        fs, fd, fsq, fn = (by_sequence(pair) for pair in (rot_c, rot_s, rot_sum, qkn))
        var = sb("var", [P, SEQS, TPS])
        rstd = sb("rstd", [P, SEQS, TPS])
        gate = [sb(f"gate{i}", [P, SEQ]) for i in range(2)]
        hid = [sb(f"hid{i}", [P, SEQ]) for i in range(NCH)]
        wqkv_rows = sb("wqkv_rows", [P, P])
        wo_rows = sb("wo_rows", [P, P])
        wvT = sb("wvT", [P, P])
        woT = sb("woT", [P, P])
        hsum = sb("hsum", [P, SEQS])
        vsum = sb("vsum", [P, SEQS])

        ps = [ctx.enter_context(nc.psum_tensor(f"bank{i}", [P, 512], F32)) for i in range(3, 8)]
        qk_ps = ctx.enter_context(nc.psum_tensor("qk_ps", [P, 2, 512], F32))
        v_ps = ctx.enter_context(nc.psum_tensor("v_ps", [P, 512], F32))
        tr0, tr1, s_ps, o0_ps, o1_ps = ps
        banks = [qk_ps[:, 0, :], qk_ps[:, 1, :], v_ps[:, :], tr0[:, :], tr1[:, :], s_ps[:, :], o0_ps[:, :], o1_ps[:, :]]

        consts_in = sem("consts_in")
        consts_ready = sem("consts_ready")
        zeros_ready = sem("zeros_ready")
        vecs_in = sem("vecs_in")
        x_in = sem("x_in")
        wqkv_in = sem("wqkv_in")
        wo_in = sem("wo_in")
        w1_in = sem("w1_in")
        w2_in = sem("w2_in")
        mid_w_in = sem("mid_w_in")
        out_done = sem("out_done")
        rot_ready = sem("rot_ready")
        vec_ready = sem("vec_ready")
        wqkv_hi_ready = sem("wqkv_hi_ready")
        wqkv_split = sem("wqkv_split")
        xs_qk_staged = sem("xs_qk_staged")
        xs_qk_hi_ready = sem("xs_qk_hi_ready")
        xs_qk_ready = sem("xs_qk_ready")
        xs_v_staged = sem("xs_v_staged")
        xs_v_hi_ready = sem("xs_v_hi_ready")
        xs_v_ready = sem("xs_v_ready")
        qk_ready = sem("qk_ready")
        v_ready = sem("v_ready")
        sq_ready = sem("sq_ready")
        rot_parts = sem("rot_parts")
        rot_added = sem("rot_added")
        ss_raw = sem("ss_raw")
        ss_ready = sem("ss_ready")
        rn_ready = sem("rn_ready")
        qkn_ready = sem("qkn_ready")
        qt_ready = sem("qt_ready")
        ktp_ready = sem("ktp_ready")
        qbd_ready = sem("qbd_ready")
        k_head = sem("k_head")
        kt_ready = sem("kt_ready")
        s_ready = sem("s_ready")
        max_ready = sem("max_ready")
        dif_ready = sem("dif_ready")
        prob_ready = sem("prob_ready")
        rden_ready = sem("rden_ready")
        ptp_ready = sem("ptp_ready")
        pt_ready = sem("pt_ready")
        vn_ready = sem("vn_ready")
        vhead_in = [sem(f"vhead_in{h}") for h in range(2)]
        vs_in = [sem(f"vs_in{h}") for h in range(2)]
        vtail_in = [sem(f"vtail_in{h}") for h in range(2)]
        o_ready = sem("o_ready")
        on_ready = sem("on_ready")
        otp_ready = sem("otp_ready")
        ot_ready = sem("ot_ready")
        y_ready = sem("y_ready")
        y_added = sem("y_added")
        xa_ready = sem("xa_ready")
        x0_ready = sem("x0_ready")
        fs_ready = sem("fs_ready")
        mean_ready = sem("mean_ready")
        fd_ready = sem("fd_ready")
        fsq_ready = sem("fsq_ready")
        varp_ready = sem("varp_ready")
        var_ready = sem("var_ready")
        rstd_ready = sem("rstd_ready")
        rb_ready = sem("rb_ready")
        fn_raw = sem("fn_raw")
        fn_ready = sem("fn_ready")
        gated_ps = sem("gated_ps")
        gate_ready = sem("gate_ready")
        hid_ready = sem("hid_ready")
        fy_ready = sem("fy_ready")
        tx_ready = sem("tx_ready")
        tw_ready = sem("tw_ready")
        tw_out = sem("tw_out")
        hsum_ready = sem("hsum_ready")
        vsum_ps = sem("vsum_ps")
        vsum_ready = sem("vsum_ready")
        ymid_ps = sem("ymid_ps")


        def first_ln(p):
            return LN_PASS * p

        def tile_after_next(t):
            return not isinstance(t, int) or t + 2 < TILES

        def over_units(eng, step):
            step(0, 0, True, True, True, False, False)
            step(0, 1, True, True, True, True, False)
            with eng.Fori(1, TILES - 2) as t:
                step(t, 0, True, True, True, True, True)
                step(t, 1, True, True, True, True, True)
            step(TILES - 2, 0, True, True, True, True, True)
            step(TILES - 2, 1, True, True, True, True, True)
            step(TILES - 1, 0, False, True, True, True, True)
            step(TILES - 1, 1, False, False, True, True, True)
            step(TILES, 0, False, False, False, True, True)
            step(TILES, 1, False, False, False, False, True)

        block = ctx.enter_context(nc.Block())

        @block.sync
        def _(sp):
            for released in (*vs_in, *vtail_in):
                sp.sem_inc(released, DMA_ONE)
            sp.dma_start(xtok[:, :, :], x.rearrange("(n p) d -> p n d", p=P)).then_inc(x_in, 16)
            sp.dma_start(ident[:, :], ident_dram).then_inc(consts_in, 16)
            sp.dma_start(rot_base[:, :, :, :], rot_dram).then_inc(consts_in, 16)
            sp.dma_start(mask[:, :, :], mask_dram).then_inc(consts_in, 16)
            sp.dma_start(scales[:, :, :, :], scales_dram.unsqueeze(0).to_broadcast([P, DEPTH, 2, DH])).then_inc(vecs_in, 16)
            sp.dma_start(vecs[:, :, :], vecs_dram).then_inc(vecs_in, 16)
            sp.dma_start(wqkv_rows[:, :], w_qkv[2 * P:3 * P, :]).then_inc(mid_w_in, 16)
            sp.dma_start(wo_rows[:, :], w_o).then_inc(mid_w_in, 16)

            def shift_values(U, TG, h):
                sp.wait_ge(o_ready, U - 1 + TWO)
                sp.wait_ge(vtail_in[h], TG * 16 + DMA_ONE)
                sp.dma_start(vs[h][0:WIN, :, :], vtail[h][0:WIN, :, :]).then_inc(vhead_in[h], 16)
                sp.wait_ge(vn_ready, U + 1 + ONE)
                sp.dma_start(vs[h][WIN:P, :, :], vn[h][0:P - WIN, :, :]).then_inc(vs_in[h], 16)
                sp.wait_ge(vhead_in[h], TG * 16 + 16)
                sp.dma_start(vtail[h][0:WIN, :, :], vn[h][P - WIN:P, :, :]).then_inc(vtail_in[h], 16)

            for p in range(2):
                with sp.Fori(0, DEPTH) as l:
                    g = l + p * DEPTH
                    sp.wait_ge(wqkv_split, g + ONE)
                    sp.wait_ge(consts_ready, 1)
                    for part in range(3):
                        sp.dma_start(wqkv[:, part * INNER:(part + 1) * INNER],
                                     Wqkv[bass.ds(l, 1), :, part * INNER:(part + 1) * INNER]
                                     .rearrange("a p n -> p (a n)")).then_inc(wqkv_in, 16)
                    sp.wait_ge(y_ready, g * UNITS + ONE)
                    sp.wait_ge(consts_ready, 1)
                    sp.dma_start(wo[:, :, :, :, :].rearrange("p c g b n -> p (c g b n)"),
                                 Wo[bass.ds(l, 1), :, :].rearrange("a p n -> p (a n)")).then_inc(wo_in, 16)
                    sp.wait_ge(fy_ready, g * SEQS + ONE)
                    sp.wait_ge(consts_ready, 1)
                    sp.dma_start(w1[:, :], W1[bass.ds(l, 1), :, :].rearrange("a p n -> p (a n)")).then_inc(w1_in, 16)
                    for j, (c, n) in enumerate(CHUNKS):
                        sp.dma_start(w2[0:n, j, :], W2[bass.ds(l, 1), c:c + n, :].rearrange("a p n -> p (a n)")
                                     ).then_inc(w2_in, 16)
                    with sp.Fori(0, TILES) as t:
                        for h in range(2):
                            shift_values(g * UNITS + 2 * t + h, g * TILES + t, h)
                        sp.wait_ge(consts_ready, 1)
            sp.wait_ge(tx_ready, 2 * SEQS)
            sp.wait_ge(x0_ready, 5 * SEQS)
            sp.dma_start(out.rearrange("(n p) d -> p n d", p=P), xtok[:, :, :]).then_inc(out_done, 16)
            sp.wait_ge(out_done, 16)

        @block.gpsimd
        def _(pool):
            for released in (rot_added, rn_ready):
                pool.sem_inc(released, TWO)
            pool.sem_inc(wqkv_split, ONE)
            for h in range(2):
                nc.gpsimd.memset(vtail[h][:, :, :], 0.0).then_inc(zeros_ready, 1)
                nc.gpsimd.memset(qbd[h][:, :, :, :, :], 0.0).then_inc(zeros_ready, 1)
                nc.gpsimd.memset(kt[h][:, :, :], 0.0).then_inc(zeros_ready, 1)
            for h in range(2):
                nc.gpsimd.memset(vn[h][:, :, DH:DV], 1.0).then_inc(zeros_ready, 1)
            nc.gpsimd.memset(mean_mat[:, :], 1.0 / P).then_inc(zeros_ready, 1)
            nc.gpsimd.memset(one[:, :], 1.0).then_inc(zeros_ready, 1)
            nc.gpsimd.memset(minus_half[:, :], -0.5).then_inc(zeros_ready, 1)
            nc.gpsimd.memset(xa[:, :, :], 0.0).then_inc(zeros_ready, 1)
            nc.gpsimd.memset(xb[:, :, :], 0.0).then_inc(zeros_ready, 1)
            pool.wait_ge(zeros_ready, 13)

            def inverse_std(n, s):
                pool.wait_ge(var_ready, n + 1)
                nc.gpsimd.tensor_tensor(rstd[:, s, :], var[:, s, :], minus_half[:, 0:TPS], ALU.pow).then_inc(rstd_ready, 1)

            def split_weights(g):
                pool.wait_ge(wqkv_in, 48 * g + 48)
                pool.wait_ge(y_ready, g * UNITS + ONE)
                nc.gpsimd.tensor_tensor(wqkv_hi[:, :], wqkv[:, :], one[:, :].to_broadcast([P, 3 * INNER]), ALU.mult).then_inc(wqkv_hi_ready, 1)
                pool.wait_ge(wqkv_hi_ready, g + 1)
                nc.gpsimd.tensor_tensor(wqkv_lo[:, :], wqkv[:, :], wqkv_hi[:, :], ALU.subtract).then_inc(wqkv_split, 1)

            def front(U, h):
                pool.wait_ge(ss_ready, U + 1)
                pool.wait_ge(qkn_ready, U - 1 + TWO)
                nc.gpsimd.tensor_tensor(rn[h][:, :], ssc[h][:, :], minus_half[:, :], ALU.pow).then_inc(rn_ready, 1)
                pool.wait_ge(rot_parts, U + 1 + ONE)
                nc.gpsimd.tensor_tensor(rot_sum[h][:, :, :, :], rot_c[h][:, :, :, :], rot_s[h][:, :, :, :], ALU.add
                                        ).then_inc(rot_added, 1)

            for p in range(2):
                for s in range(SEQS):
                    inverse_std(first_ln(p) + s, s)
                with pool.Fori(0, DEPTH) as l:
                    g = l + p * DEPTH
                    split_weights(g)
                    front(g * UNITS, 0)
                    front(g * UNITS + 1, 1)

                    def step(t, h, qk, v, mid, back1, back2):
                        if qk:
                            front(g * UNITS + 2 * t + h + 2, h)

                    over_units(pool, step)
                    for s in range(SEQS):
                        inverse_std(first_ln(p) + SEQS + SEQS * l + s, s)
                if p == 0:
                    for s in range(SEQS):
                        inverse_std(first_ln(1) - SEQS + s, s)

        @block.scalar
        def _(act):
            for released in (vn_ready, qbd_ready, kt_ready, ot_ready):
                act.sem_inc(released, ONE)
            act.wait_ge(consts_in, 48)
            act.wait_ge(zeros_ready, 13)
            nc.scalar.activation(ident16[:, :], ident[:, :], ACT.Copy).then_inc(consts_ready, 1)
            for s in range(SEQS):
                act.wait_ge(tx_ready, s + 1)
                nc.scalar.activation(x0[:, s, :], banks[s], ACT.Copy).then_inc(x0_ready, 1)

            def ln_squares(n, s):
                act.wait_ge(fd_ready, n + 1)
                nc.scalar.activation(fsq[s][:, :], fd[s][:, :], ACT.Square).then_inc(fsq_ready, 1)

            def macaron_ln(n0):
                for s in range(SEQS):
                    ln_squares(n0 + s, s)

            def stage(t, TG, xs, hi, staged, ready):
                at = (t // TPS) * SP1 + (t % TPS) * P
                flat = xa[:, :, :].rearrange("p s n -> p (s n)")
                act.wait_ge(zeros_ready, 13)
                nc.scalar.activation(xs[0:DH, :], flat[0:DH, bass.ds(at + 1, P)], ACT.Copy)
                nc.scalar.activation(xs[DH:P, :], flat[DH:P, bass.ds(at, P)], ACT.Copy).then_inc(staged, 1)
                act.wait_ge(staged, TG + 1)
                nc.scalar.activation(hi[:, :], xs[:, :], ACT.Copy).then_inc(ready, 1)

            def squares(U):
                act.wait_ge(qk_ready, U + 1)
                act.wait_ge(ss_raw, U + ONE)
                nc.scalar.activation(sq[:, :, :, :].rearrange("p a h d -> p (a h d)"),
                                     qk_ps[:, :, :].rearrange("p a n -> p (a n)"), ACT.Square).then_inc(sq_ready, 1)

            def values(U, TG, h):
                act.wait_ge(v_ready, U + 1)
                act.wait_ge(vs_in[h], TG * 16 + DMA_ONE)
                act.wait_ge(vtail_in[h], TG * 16 + DMA_ONE)
                nc.scalar.activation(vn[h][:, :, 0:DH], v_ps[:, :].rearrange("p (h d) -> p h d", d=DH), ACT.Copy).then_inc(vn_ready, 1)

            def queries(U, h):
                act.wait_ge(qt_ready, U + 1)
                for hp in range(2):
                    rows = slice(hp * DH, (hp + 1) * DH)
                    last = nc.scalar.activation(
                        qbd[h][rows, :, :, hp, :].rearrange("p a w q -> p (a w) q"),
                        tr0[rows, :].rearrange("p (aw q) -> p aw q", q=WIN), ACT.Copy)
                last.then_inc(qbd_ready, 1)

            def keys(U, h):
                nc.scalar.activation(kt[h][:, :, 0:WIN], kt[h][:, :, P:P + WIN], ACT.Copy).then_inc(k_head, 1)
                act.wait_ge(ktp_ready, U + 1)
                act.wait_ge(k_head, U + 1)
                nc.scalar.activation(kt[h][:, :, WIN:WIN + P], tr1[:, :].rearrange("p (a n) -> p a n", a=PAIRS),
                                     ACT.Copy).then_inc(kt_ready, 1)

            def exps(U, h):
                act.wait_ge(dif_ready, U + 1 + ONE)
                nc.scalar.activation(prob[h][:, :, :], dif[h][:, :, :], ACT.Exp, scale=QK_SCALE).then_inc(prob_ready, 1)

            for p in range(2):
                macaron_ln(first_ln(p))
                with act.Fori(0, DEPTH) as l:
                    g = l + p * DEPTH
                    act.wait_ge(xa_ready, first_ln(p) + SEQS + SEQS * l)
                    stage(0, g * TILES, xs_qk, xs_qk_hi, xs_qk_staged, xs_qk_hi_ready)
                    stage(0, g * TILES, xs_v, xs_v_hi, xs_v_staged, xs_v_hi_ready)
                    squares(g * UNITS)
                    squares(g * UNITS + 1)
                    stage(1, g * TILES + 1, xs_qk, xs_qk_hi, xs_qk_staged, xs_qk_hi_ready)

                    def step(t, h, qk, v, mid, back1, back2):
                        U = g * UNITS + 2 * t + h
                        if mid:
                            queries(U, h)
                        if back1:
                            exps(U - 1, 1 - h)
                        if mid:
                            keys(U, h)
                        if qk:
                            squares(U + 2)
                        if back1:
                            act.wait_ge(ptp_ready, U)
                            nc.scalar.activation(pt[1 - h][:, :, :].rearrange("p a n -> p (a n)"), tr0[:, :],
                                                 ACT.Copy).then_inc(pt_ready, 1)
                        if qk and h == 1 and tile_after_next(t):
                            stage(t + 2, g * TILES + t + 2, xs_qk, xs_qk_hi, xs_qk_staged, xs_qk_hi_ready)
                        if mid:
                            values(U, g * TILES + t, h)
                        if v and h == 1:
                            stage(t + 1, g * TILES + t + 1, xs_v, xs_v_hi, xs_v_staged, xs_v_hi_ready)
                        if back2:
                            act.wait_ge(otp_ready, U - 1)
                            nc.scalar.activation(ot[h][:, :, :, :, :, :].rearrange("p a b c d q -> p (a b c d q)"),
                                                 tr1[:, :], ACT.Copy).then_inc(ot_ready, 1)

                    over_units(act, step)

                    n0 = first_ln(p) + SEQS + SEQS * l
                    flat = xb
                    for s in range(SEQS):
                        act.wait_ge(y_added, g * UNITS + UNITS // SEQS * (s + 1) + ONE)
                        nc.scalar.activation(fs[s][0:DH, :], xb[0:DH, s, 1:SP1], ACT.Copy)
                        nc.scalar.activation(fs[s][DH:P, :], xb[DH:P, s, 0:SEQ], ACT.Copy).then_inc(fs_ready, 1)
                    for s in range(SEQS):
                        ln_squares(n0 + s, s)
                    act.wait_ge(vec_ready, g + 1)
                    for s in range(SEQS):
                        act.wait_ge(fn_raw, g * SEQS + s + 1)
                        nc.scalar.activation(fn[s][:, :], fd[s][:, :], ACT.Identity, bias=vec[:, 1:2], scale=vec[:, 0:1]
                                             ).then_inc(fn_ready, 1)
                    for s in range(SEQS):
                        for j, (c, m) in enumerate(CHUNKS):
                            i = s * NCH + j
                            act.wait_ge(gated_ps, g * SEQS * NCH + i + 1)
                            if i >= 2:
                                act.wait_ge(hid_ready, g * SEQS * NCH + i - 1)
                            nc.scalar.activation(gate[i % 2][0:m, :], banks[2 * (i % 2) + 1][0:m, :], ACT.Gelu,
                                                 bias=vec[0:m, 3 + NCH + j:4 + NCH + j]).then_inc(gate_ready, 1)
                if p == 0:
                    macaron_ln(first_ln(1) - SEQS)
                    act.wait_ge(tw_ready, 1)
                    nc.scalar.activation(wvT[:, :], banks[0][:, 0:P], ACT.Copy)
                    nc.scalar.activation(woT[:, :], banks[0][:, P:2 * P], ACT.Copy).then_inc(tw_out, 1)
                    act.wait_ge(vsum_ps, 1)
                    nc.scalar.activation(vsum[:, :], banks[1][:, 0:SEQS], ACT.Copy).then_inc(vsum_ready, 1)
            for s in range(SEQS):
                act.wait_ge(tx_ready, SEQS + s + 1)
                nc.scalar.activation(xtok[:, s * TPS:(s + 1) * TPS, :].rearrange("p n d -> p (n d)"), banks[s],
                                     ACT.Copy).then_inc(x0_ready, 1)

        @block.vector
        def _(dve):
            dve.sem_inc(qkn_ready, TWO)
            for released in (ss_raw, y_added, rot_parts, dif_ready, on_ready):
                dve.sem_inc(released, ONE)
            dve.wait_ge(vecs_in, 32)
            dve.wait_ge(consts_ready, 1)
            dve.wait_ge(zeros_ready, 13)

            def centre(n, s, src):
                dve.wait_ge(mean_ready, n + 1)
                nc.vector.tensor_tensor(fd[s][:, :], src, banks[s % 2], ALU.subtract).then_inc(fd_ready, 1)

            def ln_variance(n, s):
                dve.wait_ge(varp_ready, n + 1)
                nc.vector.tensor_scalar(var[:, s, :], banks[2 + s % 2][:, 0:TPS], EPS, None, ALU.add).then_inc(var_ready, 1)

            def macaron_ln(n0):
                for s in range(SEQS):
                    centre(n0 + s, s, x0[:, s, :])
                for s in range(SEQS):
                    ln_variance(n0 + s, s)
                for s in range(SEQS):
                    dve.wait_ge(rb_ready, n0 + s + 1)
                    nc.vector.tensor_tensor(xa[:, s, 1:SP1], fd[s][:, :], banks[4 + s % 2], ALU.mult).then_inc(xa_ready, 1)

            def split_qk_tile(TG):
                dve.wait_ge(xs_qk_hi_ready, TG + 1)
                nc.vector.tensor_tensor(xs_qk_lo[:, :], xs_qk[:, :], xs_qk_hi[:, :], ALU.subtract).then_inc(xs_qk_ready, 1)

            def split_v_tile(TG):
                dve.wait_ge(xs_v_hi_ready, TG + 1)
                nc.vector.tensor_tensor(xs_v_lo[:, :], xs_v[:, :], xs_v_hi[:, :], ALU.subtract).then_inc(xs_v_ready, 1)

            def rotate(U, t, h):
                dve.wait_ge(rot_added, U - 1 + TWO)
                tt = t % TPS
                src = qk_ps[:, :, :].rearrange("p a (h d) -> p a h d", d=DH)
                tab = rot[:, :, :, :, :].rearrange("p t c a d -> p (t c a d)")

                def part(c, lo, n):
                    v = tab[:, bass.ds(tt * (4 * DH) + c * 2 * DH, 2 * DH)].rearrange("p (a d) -> p a d", a=2)
                    return v[:, :, lo:lo + n].unsqueeze(2).to_broadcast([P, 2, UH, n])

                nc.vector.tensor_tensor(rot_c[h][:, :, :, :], src, part(0, 0, DH), ALU.mult)
                H2 = DH // 2
                for lo in (0, H2):
                    to = H2 - lo
                    last = nc.vector.tensor_tensor(rot_s[h][:, :, :, to:to + H2], src[:, :, :, lo:lo + H2],
                                                   part(1, lo, H2), ALU.mult)
                last.then_inc(rot_parts, 1)

            def square_sums(U, h):
                dve.wait_ge(sq_ready, U + 1)
                nc.vector.tensor_reduce(ss[:, :], sq[:, :, :, :].rearrange("p a h d -> p (a h) d"), AX_X, ALU.add
                                        ).then_inc(ss_raw, 1)
                dve.wait_ge(ss_raw, U + 1 + ONE)
                dve.wait_ge(rn_ready, U - 1 + TWO)
                nc.vector.tensor_scalar(ssc[h][:, :], ss[:, :], NORM_FLOOR, None, ALU.max).then_inc(ss_ready, 1)

            def normalise(U, h):
                dve.wait_ge(rot_added, U + 1 + TWO)
                dve.wait_ge(rn_ready, U + 1 + TWO)
                nc.vector.tensor_tensor(qkn[h][:, :, :, :].rearrange("p a h d -> p (a h) d"),
                                        rot_sum[h][:, :, :, :].rearrange("p a h d -> p (a h) d"),
                                        rn[h][:, :].unsqueeze(2).to_broadcast([P, 2 * UH, DH]), ALU.mult
                                        ).then_inc(qkn_ready, 1)

            def softmax_front(U, h):
                dve.wait_ge(s_ready, U + 1)
                sc = s_ps[:, :].rearrange("p (a k) -> p a k", k=KEYS)
                nc.vector.tensor_reduce(row_max[h][:, :], sc, AX_X, ALU.max).then_inc(max_ready, 1)
                dve.wait_ge(max_ready, U + 1)
                nc.vector.tensor_tensor(dif[h][:, :, :], sc, row_max[h][:, :].unsqueeze(2)
                                        .to_broadcast([P, 2 * PAIRS, KEYS]), ALU.subtract).then_inc(dif_ready, 1)

            def output_norm(U, h):
                dve.wait_ge(o_ready, U + 1 + TWO)
                o = [x[:, 0:PAIRS * DV].rearrange("p (a d) -> p a d", d=DV) for x in (o0_ps, o1_ps)]
                for gg in range(2):
                    last = nc.vector.reciprocal(rden[:, gg, :].unsqueeze(2), o[gg][:, :, DH:DV])
                last.then_inc(rden_ready, 1)
                dve.wait_ge(rden_ready, U + 1)
                for gg in range(2):
                    last = nc.vector.tensor_tensor(on[h][:, gg, :, :], o[gg][:, :, 0:DH],
                                                   rden[:, gg, :].unsqueeze(2).to_broadcast([P, PAIRS, DH]), ALU.mult)
                last.then_inc(on_ready, 1)

            def add_output(U, t, h):
                dve.wait_ge(y_ready, U + 1 + ONE)
                dve.wait_ge(y_added, U + ONE)
                at = (t // TPS) * SP1 + (t % TPS) * P + 1
                base = (xb if h else xa)[:, :, :].rearrange("p s n -> p (s n)")
                to = xb[:, :, :].rearrange("p s n -> p (s n)")
                nc.vector.tensor_tensor(to[:, bass.ds(at, P)], v_ps[:, 0:P], base[:, bass.ds(at, P)], ALU.add
                                        ).then_inc(y_added, 1)

            for p in range(2):
                if p == 0:
                    dve.wait_ge(x0_ready, SEQS)
                macaron_ln(first_ln(p))
                with dve.Fori(0, DEPTH) as l:
                    g = l + p * DEPTH
                    dve.wait_ge(xa_ready, first_ln(p) + SEQS + SEQS * l)
                    sc = scales[:, :, :, :].rearrange("p l a d -> p (l a d)")[:, bass.ds(l * (2 * DH), 2 * DH)]
                    nc.vector.tensor_tensor(rot[:, :, :, :, :].rearrange("p t c a d -> p (t c) (a d)"),
                                            rot_base[:, :, :, :].rearrange("p t a d -> p t (a d)"),
                                            sc.unsqueeze(1).to_broadcast([P, 2 * TPS, 2 * DH]), ALU.mult
                                            ).then_inc(rot_ready, 1)
                    NV = 3 + 2 * NCH
                    nc.vector.tensor_copy(vec[:, :], vecs[:, :, :].rearrange("p l v -> p (l v)")[:, bass.ds(l * NV, NV)]
                                          ).then_inc(vec_ready, 1)
                    dve.wait_ge(rot_ready, g + 1)
                    split_qk_tile(g * TILES)
                    split_v_tile(g * TILES)
                    square_sums(g * UNITS, 0)
                    rotate(g * UNITS, 0, 0)
                    square_sums(g * UNITS + 1, 1)
                    rotate(g * UNITS + 1, 0, 1)
                    split_qk_tile(g * TILES + 1)
                    normalise(g * UNITS, 0)

                    def step(t, h, qk, v, mid, back1, back2):
                        U = g * UNITS + 2 * t + h
                        if v:
                            normalise(U + 1, 1 - h)
                        if qk:
                            square_sums(U + 2, h)
                            rotate(U + 2, t + 1, h)
                        if mid:
                            softmax_front(U, h)
                        if qk and h == 1 and tile_after_next(t):
                            split_qk_tile(g * TILES + t + 2)
                        if v and h == 1:
                            split_v_tile(g * TILES + t + 1)
                        if back1:
                            output_norm(U - 1, 1 - h)
                        if back2:
                            add_output(U - 2, t - 1, h)

                    over_units(dve, step)

                    n0 = first_ln(p) + SEQS + SEQS * l
                    for s in range(SEQS):
                        centre(n0 + s, s, fs[s][:, :])
                    for s in range(SEQS):
                        ln_variance(n0 + s, s)
                    for s in range(SEQS):
                        dve.wait_ge(rb_ready, n0 + s + 1)
                        dve.wait_ge(fsq_ready, n0 + s + 1)
                        nc.vector.tensor_tensor(fd[s][:, :], fd[s][:, :], banks[4 + s % 2], ALU.mult).then_inc(fn_raw, 1)
                    for s in range(SEQS):
                        for j, (c, m) in enumerate(CHUNKS):
                            i = s * NCH + j
                            dve.wait_ge(gate_ready, g * SEQS * NCH + i + 1)
                            nc.vector.scalar_tensor_tensor(
                                hid[j][0:m, :], banks[2 * (i % 2)][0:m, :], vec[0:m, 3 + j:4 + j], gate[i % 2][0:m, :],
                                ALU.add, ALU.mult).then_inc(hid_ready, 1)
                        dve.wait_ge(fy_ready, g * SEQS + s + 1 + ONE)
                        nc.vector.scalar_tensor_tensor(
                            xa[:, s, 1:SP1], banks[6 + s % 2], vec[:, 2:3], xb[:, s, 1:SP1], ALU.add, ALU.add
                        ).then_inc(xa_ready, 1)
                dve.wait_ge(xa_ready, first_ln(p) + SEQS + SEQS * DEPTH)
                for s in range(SEQS):
                    nc.vector.scalar_tensor_tensor(x0[:, s, :], xa[:, s, 1:SP1], 0.5, x0[:, s, :], ALU.mult, ALU.add
                                                   ).then_inc(x0_ready, 1)
                if p == 0:
                    dve.wait_ge(x0_ready, 2 * SEQS)
                    macaron_ln(first_ln(1) - SEQS)
                    dve.wait_ge(xa_ready, first_ln(1))
                    nc.vector.tensor_reduce(hsum[:, :], xa[:, :, 1:SP1], AX_X, ALU.add).then_inc(hsum_ready, 1)
                    dve.wait_ge(ymid_ps, 1)
                    nc.vector.tensor_tensor(x0[:, :, :], x0[:, :, :],
                                            banks[2][:, 0:SEQS].unsqueeze(2).to_broadcast([P, SEQS, SEQ]), ALU.add
                                            ).then_inc(x0_ready, SEQS)
                    dve.wait_ge(x0_ready, 3 * SEQS)

        @block.tensor
        def _(pe):
            for released in (y_ready, fy_ready):
                pe.sem_inc(released, ONE)
            pe.sem_inc(o_ready, TWO)
            pe.wait_ge(consts_in, 48)
            pe.wait_ge(x_in, 16)
            pe.wait_ge(mid_w_in, 32)
            for s in range(SEQS):
                for j in range(TPS):
                    last = nc.tensor.transpose(banks[s][:, j * P:(j + 1) * P], xtok[:, s * TPS + j, :], ident[:, :])
                last.then_inc(tx_ready, 1)

            def ln_mean(n, s, src):
                if s >= 2:
                    pe.wait_ge(fd_ready, n - 1)
                nc.tensor.matmul(banks[s % 2], mean_mat[:, :], src, start=True, stop=True).then_inc(mean_ready, 1)

            def ln_var(n, s):
                pe.wait_ge(fsq_ready, n + 1)
                if s >= 2:
                    pe.wait_ge(var_ready, n - 1)
                for c in range(TPS):
                    last = nc.tensor.matmul(banks[2 + s % 2][:, c:c + 1], fsq[s][:, c * P:(c + 1) * P],
                                            mean_mat[:, 0:1], start=True, stop=True)
                last.then_inc(varp_ready, 1)

            def ln_spread(n, s, used, k):
                pe.wait_ge(rstd_ready, n + 1)
                if s >= 2:
                    pe.wait_ge(used, k - 1)
                for c in range(TPS):
                    last = nc.tensor.matmul(banks[4 + s % 2][:, c * P:(c + 1) * P],
                                            rstd[:, s, c:c + 1].to_broadcast([P, P]), ident[:, :], start=True, stop=True)
                last.then_inc(rb_ready, 1)

            def macaron_ln(n0):
                for s in range(SEQS):
                    ln_mean(n0 + s, s, x0[:, s, :])
                for s in range(SEQS):
                    ln_var(n0 + s, s)
                for s in range(SEQS):
                    ln_spread(n0 + s, s, xa_ready, n0 + s)

            def project(hi, lo, h, part):
                dst = (qk_ps[:, 0, :], qk_ps[:, 1, :], v_ps[:, :])[part]
                cols = slice(part * INNER + h * HALF, part * INNER + (h + 1) * HALF)
                nc.tensor.matmul(dst, hi[:, :], wqkv_hi[:, cols], start=True, stop=False)
                nc.tensor.matmul(dst, hi[:, :], wqkv_lo[:, cols], start=False, stop=False)
                return nc.tensor.matmul(dst, lo[:, :], wqkv_hi[:, cols], start=False, stop=True)

            def project_qk(U, TG, h):
                pe.wait_ge(xs_qk_ready, TG + 1)
                pe.wait_ge(rot_parts, U + ONE)
                project(xs_qk_hi, xs_qk_lo, h, 0)
                project(xs_qk_hi, xs_qk_lo, h, 1).then_inc(qk_ready, 1)

            def project_v(U, TG, h, Y):
                pe.wait_ge(xs_v_ready, TG + 1)
                pe.wait_ge(vn_ready, U + ONE)
                if Y is not None:
                    pe.wait_ge(y_added, Y + 1 + ONE)
                project(xs_v_hi, xs_v_lo, h, 2).then_inc(v_ready, 1)

            def heads_major(U, t, h):
                pe.wait_ge(qkn_ready, U + 1 + TWO)
                pe.wait_ge(qbd_ready, U + ONE)
                if not (isinstance(t, int) and t == 0):
                    pe.wait_ge(pt_ready, U - 1)
                for a in range(PAIRS):
                    last = nc.tensor.transpose(tr0[:, a * P:(a + 1) * P],
                                               qkn[h][:, 0, 2 * a:2 * a + 2, :].rearrange("p h d -> p (h d)"), ident[:, :])
                last.then_inc(qt_ready, 1)
                pe.wait_ge(kt_ready, U + ONE)
                if not (isinstance(t, int) and t == 0):
                    pe.wait_ge(ot_ready, U - 2 + ONE)
                for a in range(PAIRS):
                    last = nc.tensor.transpose(tr1[:, a * P:(a + 1) * P],
                                               qkn[h][:, 1, 2 * a:2 * a + 2, :].rearrange("p h d -> p (h d)"), ident[:, :])
                last.then_inc(ktp_ready, 1)

            def scores(U, t, h):
                pe.wait_ge(qbd_ready, U + 1 + ONE)
                pe.wait_ge(kt_ready, U + 1 + ONE)
                pe.wait_ge(dif_ready, U + ONE)
                pe.wait_ge(consts_ready, 1)
                m = mask[:, :, :].rearrange("p t k -> p (t k)")[:, bass.ds(t * (2 * KEYS), 2 * KEYS)]
                nc.tensor.matmul(s_ps[:, :], ident16[:, :], m.unsqueeze(1).to_broadcast([P, PAIRS, 2 * KEYS]),
                                 start=True, stop=False, skip_group_check=True)
                for a in range(PAIRS):
                    for gg in range(2):
                        for ws in range(2):
                            w = 2 * gg + ws
                            last = nc.tensor.matmul(
                                s_ps[ws * 64:(ws + 1) * 64, (2 * a + gg) * KEYS:(2 * a + gg + 1) * KEYS],
                                qbd[h][:, a, w, :, :].rearrange("p b q -> p (b q)"),
                                kt[h][:, a, w * WIN:w * WIN + KEYS], start=False, stop=True, skip_group_check=True)
                last.then_inc(s_ready, 1)

            def prob_major(U, h, mid):
                pe.wait_ge(prob_ready, U + 1)
                if mid:
                    pe.wait_ge(qbd_ready, U + 2 + ONE)
                else:
                    pe.wait_ge(pt_ready, U)
                for a in range(PAIRS):
                    last = nc.tensor.transpose(tr0[:, a * P:(a + 1) * P],
                                               prob[h][:, 2 * a:2 * a + 2, :].rearrange("p g k -> p (g k)"), ident[:, :])
                last.then_inc(ptp_ready, 1)

            def out_major(U, h, mid):
                pe.wait_ge(on_ready, U + 1 + ONE)
                if mid:
                    pe.wait_ge(kt_ready, U + 3 + ONE)
                else:
                    pe.wait_ge(ot_ready, U + ONE)
                for gg in range(2):
                    for pg in range(PAIRS // 2):
                        c = gg * (PAIRS // 2) + pg
                        last = nc.tensor.transpose(tr1[:, c * P:(c + 1) * P],
                                                   on[h][:, gg, 2 * pg:2 * pg + 2, :].rearrange("p a d -> p (a d)"),
                                                   ident[:, :])
                last.then_inc(otp_ready, 1)

            def wait_to_weigh(U, TG, h):
                pe.wait_ge(pt_ready, U + 1)
                pe.wait_ge(vs_in[h], TG * 16 + 16 + DMA_ONE)
                pe.wait_ge(vhead_in[h], TG * 16 + 16)
                pe.wait_ge(on_ready, U + ONE)

            def weigh_values(h):
                for gg in range(2):
                    rows = slice(gg * KEYS, (gg + 1) * KEYS)
                    o = (o0_ps, o1_ps)[gg]
                    for a in range(PAIRS):
                        for ws in range(2):
                            for hp in range(2):
                                c = 2 * ws + hp
                                last = nc.tensor.matmul(
                                    o[c * WIN:(c + 1) * WIN, a * DV:(a + 1) * DV],
                                    pt[h][rows, a, c * WIN:(c + 1) * WIN],
                                    (vn if ws else vs)[h][rows, 2 * a + hp, :],
                                    start=True, stop=True, skip_group_check=True)
                last.then_inc(o_ready, 1)

            def project_out(U, h, last_v):
                pe.wait_ge(ot_ready, U + 1 + ONE)
                pe.wait_ge(vn_ready, last_v + ONE)
                pe.wait_ge(y_added, U + ONE)
                n = 0
                for pg in range(PAIRS // 2):
                    for hp in range(2):
                        last = nc.tensor.matmul(v_ps[:, 0:P], wo[:, h, pg, hp, :], ot[h][:, :, pg, :, hp, :],
                                                start=n == 0, stop=n == PAIRS - 1)
                        n += 1
                last.then_inc(y_ready, 1)

            for p in range(2):
                pe.wait_ge(x0_ready, SEQS if p == 0 else 3 * SEQS)
                pe.wait_ge(zeros_ready, 13)
                macaron_ln(first_ln(p))
                with pe.Fori(0, DEPTH) as l:
                    g = l + p * DEPTH
                    pe.wait_ge(xa_ready, first_ln(p) + SEQS + SEQS * l)
                    pe.wait_ge(wqkv_split, g + 1 + ONE)
                    pe.wait_ge(wo_in, 16 * g + 16)
                    project_qk(g * UNITS, g * TILES, 0)
                    project_qk(g * UNITS + 1, g * TILES, 1)

                    def step(t, h, qk, v, mid, back1, back2):
                        U = g * UNITS + 2 * t + h
                        if mid:
                            heads_major(U, t, h)
                        if qk:
                            project_qk(U + 2, g * TILES + t + 1, h)
                        if mid:
                            project_v(U, g * TILES + t, h, U - 3 if back2 else None)
                        if back1:
                            prob_major(U - 1, 1 - h, mid)
                        if back1 and not back2:
                            wait_to_weigh(U - 1, g * TILES + t - 1 + h, 1 - h)
                        if mid:
                            scores(U, t, h)
                        if back1 and back2:
                            wait_to_weigh(U - 1, g * TILES + t - 1 + h, 1 - h)
                        if back2:
                            out_major(U - 2, h, mid)
                        if back1:
                            weigh_values(1 - h)
                        if back2:
                            project_out(U - 2, h, U + 1 if mid else (g + 1) * UNITS)

                    over_units(pe, step)

                    n0 = first_ln(p) + SEQS + SEQS * l
                    pe.wait_ge(y_added, g * UNITS + UNITS + ONE)
                    for s in range(SEQS):
                        pe.wait_ge(fs_ready, g * SEQS + s + 1)
                        ln_mean(n0 + s, s, fs[s][:, :])
                    for s in range(SEQS):
                        ln_var(n0 + s, s)
                    for s in range(SEQS):
                        ln_spread(n0 + s, s, fn_raw, g * SEQS + s)
                    pe.wait_ge(w1_in, 16 * g + 16)
                    pe.wait_ge(w2_in, 16 * NCH * g + 16 * NCH)

                    def down(s):
                        for j, (c, m) in enumerate(CHUNKS):
                            pe.wait_ge(hid_ready, g * SEQS * NCH + s * NCH + j + 1)
                            if j == 0 and s >= 2:
                                pe.wait_ge(xa_ready, n0 + s - 1)
                            last = nc.tensor.matmul(banks[6 + s % 2], w2[0:m, j, :], hid[j][0:m, :],
                                                    start=j == 0, stop=j == NCH - 1)
                        last.then_inc(fy_ready, 1)

                    for s in range(SEQS):
                        pe.wait_ge(fn_ready, g * SEQS + s + 1)
                        for j, (c, m) in enumerate(CHUNKS):
                            i = s * NCH + j
                            if i >= 2:
                                pe.wait_ge(hid_ready, g * SEQS * NCH + i - 1)
                            for part in range(2):
                                last = nc.tensor.matmul(banks[2 * (i % 2) + part][0:m, :],
                                                        w1[:, part * HID + c:part * HID + c + m], fn[s][:, :],
                                                        start=True, stop=True)
                            last.then_inc(gated_ps, 1)
                        down(s)
                pe.wait_ge(x0_ready, 2 * SEQS if p == 0 else 4 * SEQS)
                if p == 0:
                    macaron_ln(first_ln(1) - SEQS)
                    pe.wait_ge(xa_ready, first_ln(1))
                    nc.tensor.transpose(banks[0][:, 0:P], wqkv_rows[:, :], ident[:, :])
                    nc.tensor.transpose(banks[0][:, P:2 * P], wo_rows[:, :], ident[:, :]).then_inc(tw_ready, 1)
                    pe.wait_ge(tw_out, 1)
                    pe.wait_ge(hsum_ready, 1)
                    nc.tensor.matmul(banks[1][:, 0:SEQS], wvT[:, :], hsum[:, :], start=True, stop=True).then_inc(vsum_ps, 1)
                    pe.wait_ge(vsum_ready, 1)
                    nc.tensor.matmul(banks[2][:, 0:SEQS], woT[:, :], vsum[:, :], start=True, stop=True).then_inc(ymid_ps, 1)
            for s in range(SEQS):
                for j in range(TPS):
                    last = nc.tensor.transpose(banks[s][:, j * P:(j + 1) * P], x0[:, s, j * P:(j + 1) * P], ident[:, :])
                last.then_inc(tx_ready, 1)


def layer_vectors(ln_g, ln_b, b1, b2):
    out = np.zeros((P, DEPTH, 3 + 2 * NCH), np.float32)
    for i, v in enumerate((ln_g, ln_b, b2)):
        out[:, :, i] = v.T
    for part in range(2):
        for j, (c, n) in enumerate(CHUNKS):
            out[0:n, :, 3 + part * NCH + j] = b1[:, part * HID + c:part * HID + c + n].T
    return out


def wo_rows_by_pair(w):
    return w.reshape(DEPTH, HEADS // 4, 2, 2, DH, P).transpose(0, 2, 4, 1, 3, 5).reshape(DEPTH, P, -1)


def kernel(**inputs):
    import ml_dtypes
    from concourse import bacc
    from concourse.bass_utils import run_bass_kernel_spmd

    given = {name.removeprefix("L0_"): np.asarray(a) for name, a in inputs.items()}
    x = given["attn_x"]
    nc = bacc.Bacc("TRN2", target_bir_lowering=False, num_devices=1)
    arrays = {
        "x_dram": x.reshape(-1, P),
        "w_qkv_dram": given["attn_w_qkv"],
        "w_o_dram": given["attn_w_o"],
        "layer_wqkv_dram": given["ffn_Wqkv"],
        "layer_wo_dram": wo_rows_by_pair(given["ffn_Wo"]),
        "layer_w1_dram": given["ffn_W1"],
        "layer_w2_dram": given["ffn_W2"],
        "layer_scales_dram": np.stack([given["ffn_q_scale"], given["ffn_k_scale"]], 1),
        "layer_vectors_dram": layer_vectors(*(given["ffn_" + n] for n in ("ln_g", "ln_b", "b1", "b2"))),
        "rotary_base_dram": rotary_base().reshape(P, TPS * 2, 2, DH),
        "score_mask_dram": score_mask().astype(ml_dtypes.bfloat16),
        "identity_dram": np.eye(P, dtype=np.float32),
    }
    arrays = {name: np.ascontiguousarray(a) for name, a in arrays.items()}
    args = [nc.dram_tensor(name, a.shape, mybir.dt.from_np(a.dtype), kind="ExternalInput").ap()
            for name, a in arrays.items()]
    out = nc.dram_tensor("out", (SEQS * SEQ, P), F32, kind="ExternalOutput").ap()
    build(nc, *args, out)
    r = run_bass_kernel_spmd(nc, [arrays], core_ids=[0])
    return r.results[0]["out"].reshape(x.shape)
```

```python
from contextlib import ExitStack

import concourse.bass as bass
import numpy as np
from concourse import mybir

F32 = mybir.dt.float32
BF16 = mybir.dt.bfloat16
F32R = mybir.dt.float32r
ALU = mybir.AluOpType
ACT = mybir.ActivationFunctionType
AX_X = mybir.AxisListType.X

P = 128
SEQS, SEQ = 4, 512
TILES = SEQS * SEQ // P
TPS = SEQ // P
DEPTH = 6
HEADS, DH = 16, 64
INNER = HEADS * DH
HALF = INNER // 2
UH = HEADS // 2
PAIRS = UH // 2
WIN = 32
WPT = P // WIN
KEYS = 2 * WIN
HID = int(P * 4 * 2 / 3)
CHUNKS = [(c, min(P, HID - c)) for c in range(0, HID, P)]
NCH = len(CHUNKS)
SP1 = SEQ + 1
UNITS = 2 * TILES
QK_SCALE = 8.0
POOL_HEADS = 6
DV = DH + 1
NORM_LIMIT = 1e12
EPS = 1e-5
MASKED = -1e30
ONE, TWO, DMA_ONE = 1, 2, 16
LN_PAIRS = [(s, s + 1) for s in range(0, SEQS, 2)]
LN_PASS = 4 + 4 * DEPTH + 4


def rotary_base():
    half = np.arange(0, DH, 2, dtype=np.float32)
    inv_freq = (1.0 / np.float32(10000.0) ** (half / np.float32(DH))).astype(np.float32)
    t = np.arange(SEQ, dtype=np.float32)
    freqs = t[:, None] * inv_freq[None, :]
    freqs = np.concatenate([freqs, freqs], -1)
    base = (half + 0.4 * DH) / (1.4 * DH)
    power = (t - SEQ // 2) / (WIN // 2)
    scale = base[None, :].astype(np.float64) ** power[:, None]
    scale = np.concatenate([scale, scale], -1)
    cos, sin = np.cos(freqs.astype(np.float64)), np.sin(freqs.astype(np.float64))
    sign = np.where(np.arange(DH) < DH // 2, 1.0, -1.0)
    out = np.empty((2, 2, SEQ, DH))
    for qk, s in enumerate((scale, 1.0 / scale)):
        out[0, qk] = cos * s
        out[1, qk] = sin * s * sign
    out = out.reshape(2, 2, TPS, P, DH).transpose(3, 2, 0, 1, 4)
    return np.ascontiguousarray(out.astype(np.float32))


def score_mask():
    ws, hp, q, tile, g, key = np.meshgrid(
        np.arange(2), np.arange(2), np.arange(WIN), np.arange(TILES), np.arange(2), np.arange(KEYS), indexing="ij")
    prev = key < WIN
    seen = np.where(prev, key >= q, key - WIN <= q)
    first = (tile % TPS == 0) & (g == 0) & (ws == 0)
    seen &= ~(first & prev)
    return np.where(seen, 0.0, MASKED).reshape(P, TILES, 2 * KEYS)


def build(nc, x, w_qkv, w_o, Wqkv, Wo, W1, W2, scales_dram, vecs_dram, rot_dram, mask_dram, ident_dram, out):
    ctx = ExitStack()
    with ctx:
        def sb(name, shape, dt=F32):
            return ctx.enter_context(nc.sbuf_tensor(name, shape, dt))

        def sem(name):
            return ctx.enter_context(nc.semaphore(name))

        ident = sb("ident", [P, P])
        ident16 = sb("ident16", [P, P], BF16)
        mean_mat = sb("mean_mat", [P, P])
        one = sb("one", [P, 1])
        minus_half = sb("minus_half", [P, UH * 2])
        mask = sb("mask", [P, TILES, 2 * KEYS], BF16)
        rot_base = sb("rot_base", [P, TPS * 2, 2, DH])
        rot = sb("rot", [P, TPS, 2, 2, DH])
        scales = sb("scales", [P, DEPTH, 2, DH])
        vecs = sb("vecs", [P, DEPTH, 3 + 2 * NCH])
        vec = sb("vec", [P, 3 + 2 * NCH])
        wqkv_hi = sb("wqkv_hi", [P, 3 * INNER], F32R)
        wqkv_lo = sb("wqkv_lo", [P, 3 * INNER], F32R)
        wo = sb("wo", [P, 2, PAIRS // 2, 2, P])
        w1 = sb("w1", [P, 2 * HID])
        w1_hi = sb("w1_hi", [P, 2 * HID], F32R)
        w1_lo = sb("w1_lo", [P, 2 * HID], F32R)
        w2 = sb("w2", [P, NCH, P])
        x0 = sb("x0", [P, SEQS, SEQ])
        xa = sb("xa", [P, SEQS, SP1])
        xb = sb("xb", [P, SEQS, SP1])
        xs_qk = sb("xs_qk", [P, P])
        xs_v = sb("xs_v", [P, P])
        xs_qk_hi, xs_qk_lo, xs_v_hi, xs_v_lo = (sb(n, [P, P], F32R) for n in ("xs_qk_hi", "xs_qk_lo", "xs_v_hi", "xs_v_lo"))
        sq = sb("sq", [P, 2, UH, DH])
        rot_c, rot_s, rot_sum = ([sb(f"{n}{h}", [P, 2, UH, DH]) for h in range(2)] for n in ("rot_c", "rot_s", "rot_sum"))
        qkn = [sb(f"qkn{h}", [P, 2, UH, DH]) for h in range(2)]
        sq_half = sb("sq_half", [P, 2 * UH, DH // 2])
        ss = [sb(f"ss{h}", [P, 2 * UH]) for h in range(2)]
        rn = [sb(f"rn{h}", [P, 2 * UH]) for h in range(2)]
        qbd = [sb(f"qbd{h}", [P, PAIRS, WPT, 2, WIN]) for h in range(2)]
        kt = [sb(f"kt{h}", [P, PAIRS, WIN + P]) for h in range(2)]
        vn = [sb(f"vn{h}", [P, UH, DV]) for h in range(2)]
        vs = [sb(f"vs{h}", [P, UH, DV]) for h in range(2)]
        vtail = [sb(f"vtail{h}", [P, UH, DV]) for h in range(2)]
        dif = [sb(f"dif{h}", [P, PAIRS * 2, KEYS]) for h in range(2)]
        prob = [sb(f"prob{h}", [P, PAIRS * 2, KEYS]) for h in range(2)]
        row_max = [sb(f"row_max{h}", [P, PAIRS * 2]) for h in range(2)]
        rden = sb("rden", [P, 2, PAIRS])
        pt = [sb(f"pt{h}", [P, PAIRS, P]) for h in range(2)]
        on = [sb(f"on{h}", [P, 2, PAIRS, DH]) for h in range(2)]
        ot = [sb(f"ot{h}", [P, 2, PAIRS // 2, 2, 2, WIN]) for h in range(2)]
        wqkv_blocks = [b.rearrange("p a k -> p (a k)") for b in (*(x[:, :, :] for x in prob), *(x[:, :, :] for x in pt))
                       ] + [x[:, :, :, :].rearrange("p g a d -> p (g a d)") for x in on]
        def by_sequence(pair):
            return [pair[s // 2][:, s % 2, :, :].rearrange("p h d -> p (h d)") for s in range(SEQS)]

        fs, fd, fsq, fn = (by_sequence(pair) for pair in (rot_c, rot_s, rot_sum, qkn))
        fn_hi, fn_lo = ([sb(f"{n}{i}", [P, SEQ], F32R) for i in range(2)] for n in ("fn_hi", "fn_lo"))
        var = sb("var", [P, SEQS, TPS])
        rstd = sb("rstd", [P, SEQS, TPS])
        gate = [b[:, :, :].rearrange("p a k -> p (a k)") for b in dif]
        hid_all = sb("hid", [P, 2, NCH, SEQ])
        hid = [[hid_all[:, i, j, :] for j in range(NCH)] for i in range(2)]
        xtok = hid_all[:, :, :, :].rearrange("p i j n -> p (i j n)")[:, 0:TILES * P].rearrange("p (n d) -> p n d", d=P)
        wqkv_rows = sb("wqkv_rows", [P, P])
        wo_rows = sb("wo_rows", [P, P])
        wvT = sb("wvT", [P, P])
        woT = sb("woT", [P, P])
        hsum = sb("hsum", [P, SEQS])
        vsum = sb("vsum", [P, SEQS])

        ps = [ctx.enter_context(nc.psum_tensor(f"bank{i}", [P, 512], F32)) for i in range(3, 6)]
        o_ps = ctx.enter_context(nc.psum_tensor("o_ps", [P, 2, 512], F32))
        qk_ps = ctx.enter_context(nc.psum_tensor("qk_ps", [P, 2, 512], F32))
        v_ps = ctx.enter_context(nc.psum_tensor("v_ps", [P, 512], F32))
        tr0, tr1, s_ps = ps
        banks = [qk_ps[:, 0, :], qk_ps[:, 1, :], v_ps[:, :], tr0[:, :], tr1[:, :], s_ps[:, :], o_ps[:, 0, :], o_ps[:, 1, :]]

        consts_in = sem("consts_in")
        consts_ready = sem("consts_ready")
        zeros_ready = sem("zeros_ready")
        vecs_in = sem("vecs_in")
        x_in = sem("x_in")
        wqkv_in = sem("wqkv_in")
        wo_in = sem("wo_in")
        w1_in = sem("w1_in")
        w2_in = sem("w2_in")
        mid_w_in = sem("mid_w_in")
        out_done = sem("out_done")
        rot_ready = sem("rot_ready")
        vec_ready = sem("vec_ready")
        wqkv_hi_ready = sem("wqkv_hi_ready")
        wqkv_split = sem("wqkv_split")
        xs_qk_staged = sem("xs_qk_staged")
        xs_qk_hi_ready = sem("xs_qk_hi_ready")
        xs_qk_ready = sem("xs_qk_ready")
        xs_v_staged = sem("xs_v_staged")
        xs_v_hi_ready = sem("xs_v_hi_ready")
        xs_v_ready = sem("xs_v_ready")
        qk_ready = sem("qk_ready")
        v_ready = sem("v_ready")
        sq_ready = sem("sq_ready")
        rot_parts = sem("rot_parts")
        rot_added = sem("rot_added")
        rot_share = sem("rot_share")
        ss_ready = sem("ss_ready")
        halved = sem("halved")
        rn_ready = sem("rn_ready")
        qkn_ready = sem("qkn_ready")
        qt_ready = sem("qt_ready")
        ktp_ready = sem("ktp_ready")
        qbd_ready = sem("qbd_ready")
        k_head = sem("k_head")
        kt_ready = sem("kt_ready")
        s_ready = sem("s_ready")
        max_ready = sem("max_ready")
        dif_ready = sem("dif_ready")
        prob_ready = sem("prob_ready")
        rden_ready = sem("rden_ready")
        ptp_ready = sem("ptp_ready")
        pt_ready = sem("pt_ready")
        vn_ready = sem("vn_ready")
        vhead_in = [sem(f"vhead_in{h}") for h in range(2)]
        vs_in = [sem(f"vs_in{h}") for h in range(2)]
        vtail_in = [sem(f"vtail_in{h}") for h in range(2)]
        o_ready = sem("o_ready")
        on_ready = sem("on_ready")
        otp_ready = sem("otp_ready")
        ot_ready = sem("ot_ready")
        y_ready = sem("y_ready")
        y_added = sem("y_added")
        xa_ready = sem("xa_ready")
        x0_ready = sem("x0_ready")
        fs_ready = sem("fs_ready")
        mean_ready = sem("mean_ready")
        fd_ready = sem("fd_ready")
        fsq_ready = sem("fsq_ready")
        varp_ready = sem("varp_ready")
        var_ready = sem("var_ready")
        rstd_ready = sem("rstd_ready")
        rb_ready = sem("rb_ready")
        fn_raw = sem("fn_raw")
        fn_whole = sem("fn_whole")
        fn_hi_ready = sem("fn_hi_ready")
        w1_hi_ready = sem("w1_hi_ready")
        w1_split = sem("w1_split")
        fn_ready = sem("fn_ready")
        gated_ps = sem("gated_ps")
        gate_ready = sem("gate_ready")
        hid_ready = sem("hid_ready")
        fy_ready = sem("fy_ready")
        tx_ready = sem("tx_ready")
        tw_ready = sem("tw_ready")
        tw_out = sem("tw_out")
        hsum_ready = sem("hsum_ready")
        vsum_ps = sem("vsum_ps")
        vsum_ready = sem("vsum_ready")
        ymid_ps = sem("ymid_ps")


        def first_ln(p):
            return LN_PASS * p

        def tile_after_next(t):
            return not isinstance(t, int) or t + 2 < TILES

        def over_units(eng, step, shift, mean, squares, variance, spread):
            step(0, 0, True, True, True, False, False)
            step(0, 1, True, True, True, True, False)
            with eng.Fori(1, TILES - 2) as t:
                step(t, 0, True, True, True, True, True)
                step(t, 1, True, True, True, True, True)
            step(TILES - 2, 0, True, True, True, True, True)
            step(TILES - 2, 1, True, True, True, True, True)
            shift(0)
            shift(1)
            mean(0)
            mean(1)
            step(TILES - 1, 0, False, True, True, True, True)
            squares(0)
            squares(1)
            step(TILES - 1, 1, False, False, True, True, True)
            variance(0)
            variance(1)
            step(TILES, 0, False, False, False, True, True)
            spread(0)
            step(TILES, 1, False, False, False, False, True)
            shift(2)
            spread(1)
            shift(3)

        def over_feed_forward(mean, squares, variance, spread, gated, down, begin, project, rotate):
            gated(0, 0)
            mean(2)
            gated(0, 1)
            mean(3)
            squares(2)
            gated(0, 2)
            squares(3)
            gated(1, 0)
            variance(2)
            down(0)
            gated(1, 1)
            variance(3)
            gated(1, 2)
            spread(2)
            begin()
            down(1)
            gated(2, 0)
            spread(3)
            gated(2, 1)
            gated(2, 2)
            project(0)
            rotate(0)
            down(2)
            gated(3, 0)
            gated(3, 1)
            project(1)
            gated(3, 2)
            rotate(1)
            down(3)

        def over_layers(eng, p, parts):
            def attention(l):
                ready, *units = parts(l, l + p * DEPTH)[3:10]
                ready()
                over_units(eng, *units)

            def feed_forward(l, following):
                over_feed_forward(*parts(l, l + p * DEPTH)[6:], *following)

            begin, project, rotate = parts(0, p * DEPTH)[:3]
            begin()
            project(0)
            rotate(0)
            project(1)
            rotate(1)
            attention(0)
            with eng.Fori(1, DEPTH) as l:
                feed_forward(l - 1, parts(l, l + p * DEPTH)[:3])
                attention(l)
            feed_forward(DEPTH - 1, (nothing, nothing, nothing))

        def nothing(*_):
            pass

        block = ctx.enter_context(nc.Block())

        @block.sync
        def _(sp):
            for released in (*vs_in, *vtail_in):
                sp.sem_inc(released, DMA_ONE)
            sp.dma_start(xtok[:, :, :], x.rearrange("(n p) d -> p n d", p=P)).then_inc(x_in, 16)
            sp.dma_start(ident[:, :], ident_dram).then_inc(consts_in, 16)
            sp.dma_start(rot_base[:, :, :, :], rot_dram).then_inc(consts_in, 16)
            sp.dma_start(mask[:, :, :], mask_dram).then_inc(consts_in, 16)
            sp.dma_start(scales[:, :, :, :], scales_dram.unsqueeze(0).to_broadcast([P, DEPTH, 2, DH])).then_inc(vecs_in, 16)
            sp.dma_start(vecs[:, :, :], vecs_dram).then_inc(vecs_in, 16)
            sp.dma_start(wqkv_rows[:, :], w_qkv[2 * P:3 * P, :]).then_inc(mid_w_in, 16)
            sp.dma_start(wo_rows[:, :], w_o).then_inc(mid_w_in, 16)

            def shift_values(U, TG, h):
                sp.wait_ge(o_ready, U - 1 + TWO)
                sp.wait_ge(vtail_in[h], TG * 16 + DMA_ONE)
                sp.dma_start(vs[h][0:WIN, :, :], vtail[h][0:WIN, :, :]).then_inc(vhead_in[h], 16)
                sp.wait_ge(vn_ready, U + 1 + ONE)
                sp.dma_start(vs[h][WIN:P, :, :], vn[h][0:P - WIN, :, :]).then_inc(vs_in[h], 16)
                sp.wait_ge(vhead_in[h], TG * 16 + 16)
                sp.dma_start(vtail[h][0:WIN, :, :], vn[h][P - WIN:P, :, :]).then_inc(vtail_in[h], 16)

            for p in range(2):
                with sp.Fori(0, DEPTH) as l:
                    g = l + p * DEPTH
                    sp.wait_ge(y_ready, g * UNITS + ONE)
                    sp.wait_ge(consts_ready, 1)
                    for b, staged in enumerate(wqkv_blocks):
                        sp.dma_start(staged, Wqkv[bass.ds(l, 1), :, b * HALF:(b + 1) * HALF]
                                     .rearrange("a p n -> p (a n)")).then_inc(wqkv_in, 16)
                    sp.dma_start(wo[:, :, :, :, :].rearrange("p c g b n -> p (c g b n)"),
                                 Wo[bass.ds(l, 1), :, :].rearrange("a p n -> p (a n)")).then_inc(wo_in, 16)
                    sp.wait_ge(fy_ready, g * SEQS + ONE)
                    sp.wait_ge(consts_ready, 1)
                    sp.dma_start(w1[:, :], W1[bass.ds(l, 1), :, :].rearrange("a p n -> p (a n)")).then_inc(w1_in, 16)
                    for j, (c, n) in enumerate(CHUNKS):
                        sp.dma_start(w2[0:n, j, :], W2[bass.ds(l, 1), c:c + n, :].rearrange("a p n -> p (a n)")
                                     ).then_inc(w2_in, 16)
                    with sp.Fori(0, TILES) as t:
                        for h in range(2):
                            shift_values(g * UNITS + 2 * t + h, g * TILES + t, h)
                        sp.wait_ge(consts_ready, 1)
            sp.wait_ge(tx_ready, 2 * SEQS)
            sp.wait_ge(x0_ready, 5 * SEQS)
            sp.dma_start(out.rearrange("(n p) d -> p n d", p=P), xtok[:, :, :]).then_inc(out_done, 16)
            sp.wait_ge(out_done, 16)

        @block.gpsimd
        def _(pool):
            for released in (rot_added, rn_ready):
                pool.sem_inc(released, TWO)
            for released in (wqkv_split, w1_split, halved):
                pool.sem_inc(released, ONE)
            for h in range(2):
                nc.gpsimd.memset(vtail[h][:, :, :], 0.0).then_inc(zeros_ready, 1)
                nc.gpsimd.memset(qbd[h][:, :, :, :, :], 0.0).then_inc(zeros_ready, 1)
                nc.gpsimd.memset(kt[h][:, :, :], 0.0).then_inc(zeros_ready, 1)
            for h in range(2):
                nc.gpsimd.memset(vn[h][:, :, DH:DV], 1.0).then_inc(zeros_ready, 1)
            nc.gpsimd.memset(mean_mat[:, :], 1.0 / P).then_inc(zeros_ready, 1)
            nc.gpsimd.memset(one[:, :], 1.0).then_inc(zeros_ready, 1)
            nc.gpsimd.memset(minus_half[:, :], -0.5).then_inc(zeros_ready, 1)
            nc.gpsimd.memset(xa[:, :, :], 0.0).then_inc(zeros_ready, 1)
            nc.gpsimd.memset(xb[:, :, :], 0.0).then_inc(zeros_ready, 1)
            pool.wait_ge(zeros_ready, 13)

            def inverse_std(n, s):
                pool.wait_ge(var_ready, n + 1)
                nc.gpsimd.tensor_tensor(rstd[:, s, :], var[:, s, :], minus_half[:, 0:TPS], ALU.pow).then_inc(rstd_ready, 1)

            def split_high(g):
                pool.wait_ge(y_ready, g * UNITS + ONE)
                pool.wait_ge(wqkv_in, 16 * len(wqkv_blocks) * (g + 1))
                for b, staged in enumerate(wqkv_blocks):
                    nc.gpsimd.tensor_tensor(wqkv_hi[:, b * HALF:(b + 1) * HALF], staged, one[:, :].to_broadcast([P, HALF]),
                                            ALU.mult).then_inc(wqkv_hi_ready, 1)

            def split_low(g):
                pool.wait_ge(wqkv_hi_ready, len(wqkv_blocks) * (g + 1))
                for b, staged in enumerate(wqkv_blocks):
                    last = nc.gpsimd.tensor_tensor(wqkv_lo[:, b * HALF:(b + 1) * HALF], staged,
                                                   wqkv_hi[:, b * HALF:(b + 1) * HALF], ALU.subtract)
                last.then_inc(wqkv_split, 1)

            def split_w1(g):
                pool.wait_ge(w1_in, 16 * g + 16)
                pool.wait_ge(fy_ready, g * SEQS + ONE)
                nc.gpsimd.tensor_tensor(w1_hi[:, :], w1[:, :], one[:, :].to_broadcast([P, 2 * HID]), ALU.mult
                                        ).then_inc(w1_hi_ready, 1)
                pool.wait_ge(w1_hi_ready, g + 1)
                nc.gpsimd.tensor_tensor(w1_lo[:, :], w1[:, :], w1_hi[:, :], ALU.subtract).then_inc(w1_split, 1)

            def front(U, h):
                pool.wait_ge(sq_ready, U + 1)
                pool.wait_ge(ss_ready, U + ONE)
                folded = sq[:, :, :, :].rearrange("p a h d -> p (a h) d")
                nc.gpsimd.tensor_tensor(sq_half[:, :, :], folded[:, :, 0:DH // 2], folded[:, :, DH // 2:DH], ALU.add
                                        ).then_inc(halved, 1)
                pool.wait_ge(ss_ready, U + 1 + ONE)
                pool.wait_ge(qkn_ready, U - 1 + TWO)
                nc.gpsimd.tensor_tensor(rn[h][:, :], ss[h][:, :], minus_half[:, :], ALU.pow).then_inc(rn_ready, 1)
                pool.wait_ge(rot_parts, U + 1 + ONE)
                nc.gpsimd.tensor_tensor(*(b[h][:, :, 0:POOL_HEADS, :] for b in (rot_sum, rot_c, rot_s)), ALU.add
                                        ).then_inc(rot_added, 1)

            for p in range(2):
                for s in range(SEQS):
                    inverse_std(first_ln(p) + s, s)

                def attention(l):
                    g = l + p * DEPTH
                    front(g * UNITS, 0)
                    front(g * UNITS + 1, 1)

                    def step(t, h, qk, v, mid, back1, back2):
                        if qk:
                            front(g * UNITS + 2 * t + h + 2, h)

                    def mean(s):
                        if s == 0:
                            split_w1(g)

                    def variance(s):
                        inverse_std(first_ln(p) + SEQS + SEQS * l + s, s)

                    over_units(pool, step, nothing, mean, nothing, variance, nothing)

                def last_stds(l):
                    for s in (2, 3):
                        inverse_std(first_ln(p) + SEQS + SEQS * l + s, s)

                split_high(p * DEPTH)
                split_low(p * DEPTH)
                attention(0)
                with pool.Fori(1, DEPTH) as l:
                    split_high(l + p * DEPTH)
                    last_stds(l - 1)
                    split_low(l + p * DEPTH)
                    attention(l)
                last_stds(DEPTH - 1)
                if p == 0:
                    for s in range(SEQS):
                        inverse_std(first_ln(1) - SEQS + s, s)

        @block.scalar
        def _(act):
            for released in (vn_ready, qbd_ready, kt_ready, ot_ready):
                act.sem_inc(released, ONE)
            act.wait_ge(consts_in, 48)
            act.wait_ge(zeros_ready, 13)
            nc.scalar.activation(ident16[:, :], ident[:, :], ACT.Copy).then_inc(consts_ready, 1)
            for s in range(SEQS):
                act.wait_ge(tx_ready, s + 1)
                nc.scalar.activation(x0[:, s, :], banks[s], ACT.Copy).then_inc(x0_ready, 1)

            def ln_squares(n, s):
                act.wait_ge(fd_ready, n + 1)
                nc.scalar.activation(fsq[s][:, :], fd[s][:, :], ACT.Square).then_inc(fsq_ready, 1)

            def macaron_ln(n0):
                for s in range(SEQS):
                    ln_squares(n0 + s, s)

            def stage(t, TG, xs, hi, staged, ready):
                at = (t // TPS) * SP1 + (t % TPS) * P
                flat = xa[:, :, :].rearrange("p s n -> p (s n)")
                act.wait_ge(zeros_ready, 13)
                nc.scalar.activation(xs[0:DH, :], flat[0:DH, bass.ds(at + 1, P)], ACT.Copy)
                nc.scalar.activation(xs[DH:P, :], flat[DH:P, bass.ds(at, P)], ACT.Copy).then_inc(staged, 1)
                act.wait_ge(staged, TG + 1)
                nc.scalar.activation(hi[:, :], xs[:, :], ACT.Copy).then_inc(ready, 1)

            def squares(U):
                act.wait_ge(qk_ready, U + 1)
                act.wait_ge(halved, U + ONE)
                nc.scalar.activation(sq[:, :, :, :].rearrange("p a h d -> p (a h d)"),
                                     qk_ps[:, :, :].rearrange("p a n -> p (a n)"), ACT.Square).then_inc(sq_ready, 1)

            def values(U, TG, h):
                act.wait_ge(v_ready, U + 1)
                act.wait_ge(vs_in[h], TG * 16 + DMA_ONE)
                act.wait_ge(vtail_in[h], TG * 16 + DMA_ONE)
                nc.scalar.activation(vn[h][:, :, 0:DH], v_ps[:, :].rearrange("p (h d) -> p h d", d=DH), ACT.Copy).then_inc(vn_ready, 1)

            def queries(U, h):
                act.wait_ge(qt_ready, U + 1)
                for hp in range(2):
                    rows = slice(hp * DH, (hp + 1) * DH)
                    last = nc.scalar.activation(
                        qbd[h][rows, :, :, hp, :].rearrange("p a w q -> p (a w) q"),
                        tr0[rows, :].rearrange("p (aw q) -> p aw q", q=WIN), ACT.Copy)
                last.then_inc(qbd_ready, 1)

            def last_keys(h):
                nc.scalar.activation(kt[h][:, :, 0:WIN], kt[h][:, :, P:P + WIN], ACT.Copy).then_inc(k_head, 1)

            def keys(U, h):
                act.wait_ge(ktp_ready, U + 1)
                act.wait_ge(k_head, U + 1)
                nc.scalar.activation(kt[h][:, :, WIN:WIN + P], tr1[:, :].rearrange("p (a n) -> p a n", a=PAIRS),
                                     ACT.Copy).then_inc(kt_ready, 1)

            def exps(U, h):
                act.wait_ge(dif_ready, U + 1 + ONE)
                nc.scalar.activation(prob[h][:, :, :], dif[h][:, :, :], ACT.Exp, scale=QK_SCALE).then_inc(prob_ready, 1)

            for p in range(2):
                macaron_ln(first_ln(p))

                def parts(l, g):
                    def begin():
                        act.wait_ge(xa_ready, first_ln(p) + SEQS * l + 1)
                        stage(0, g * TILES, xs_qk, xs_qk_hi, xs_qk_staged, xs_qk_hi_ready)
                        stage(0, g * TILES, xs_v, xs_v_hi, xs_v_staged, xs_v_hi_ready)

                    def first_squares(u):
                        squares(g * UNITS + u)
                        if u == 1:
                            stage(1, g * TILES + 1, xs_qk, xs_qk_hi, xs_qk_staged, xs_qk_hi_ready)

                    def ready():
                        act.wait_ge(xa_ready, first_ln(p) + SEQS + SEQS * l)

                    def step(t, h, qk, v, mid, back1, back2):
                        U = g * UNITS + 2 * t + h
                        if mid:
                            last_keys(h)
                            queries(U, h)
                        if back1:
                            exps(U - 1, 1 - h)
                        if mid:
                            keys(U, h)
                        if qk:
                            squares(U + 2)
                        if back1:
                            act.wait_ge(ptp_ready, U)
                            nc.scalar.activation(pt[1 - h][:, :, :].rearrange("p a n -> p (a n)"), tr0[:, :],
                                                 ACT.Copy).then_inc(pt_ready, 1)
                        if qk and h == 1 and tile_after_next(t):
                            stage(t + 2, g * TILES + t + 2, xs_qk, xs_qk_hi, xs_qk_staged, xs_qk_hi_ready)
                        if mid:
                            values(U, g * TILES + t, h)
                        if v and h == 1:
                            stage(t + 1, g * TILES + t + 1, xs_v, xs_v_hi, xs_v_staged, xs_v_hi_ready)
                        if back2:
                            act.wait_ge(otp_ready, U - 1)
                            nc.scalar.activation(ot[h][:, :, :, :, :, :].rearrange("p a b c d q -> p (a b c d q)"),
                                                 tr1[:, :], ACT.Copy).then_inc(ot_ready, 1)

                    n0 = first_ln(p) + SEQS + SEQS * l

                    def shift(s):
                        if s == 0:
                            act.wait_ge(qkn_ready, g * UNITS + UNITS - 1 + TWO)
                        act.wait_ge(y_added, g * UNITS + UNITS // SEQS * (s + 1) + ONE)
                        nc.scalar.activation(fs[s][0:DH, :], xb[0:DH, s, 1:SP1], ACT.Copy)
                        nc.scalar.activation(fs[s][DH:P, :], xb[DH:P, s, 0:SEQ], ACT.Copy).then_inc(fs_ready, 1)

                    def normed_squares(s):
                        ln_squares(n0 + s, s)

                    def spread(s):
                        act.wait_ge(vec_ready, g + 1)
                        act.wait_ge(fn_raw, g * SEQS + s + 1)
                        nc.scalar.activation(fn[s][:, :], fd[s][:, :], ACT.Identity, bias=vec[:, 1:2], scale=vec[:, 0:1]
                                             ).then_inc(fn_whole, 1)
                        act.wait_ge(fn_whole, g * SEQS + s + 1)
                        if s >= 2:
                            act.wait_ge(gated_ps, g * SEQS * NCH + (s - 1) * NCH)
                        nc.scalar.activation(fn_hi[s % 2][:, :], fn[s][:, :], ACT.Copy).then_inc(fn_hi_ready, 1)

                    def gated(s, j):
                        i, (c, m) = s * NCH + j, CHUNKS[j]
                        act.wait_ge(gated_ps, g * SEQS * NCH + i + 1)
                        if i >= 2:
                            act.wait_ge(hid_ready, g * SEQS * NCH + i - 1)
                        nc.scalar.activation(gate[i % 2][0:m, :], banks[3 + 2 * (i % 2)][0:m, :], ACT.Gelu,
                                             bias=vec[0:m, 3 + NCH + j:4 + NCH + j]).then_inc(gate_ready, 1)

                    return (begin, nothing, first_squares, ready, step, shift, nothing, normed_squares, nothing, spread, gated, nothing)

                over_layers(act, p, parts)
                if p == 0:
                    macaron_ln(first_ln(1) - SEQS)
                    act.wait_ge(tw_ready, 1)
                    nc.scalar.activation(wvT[:, :], banks[0][:, 0:P], ACT.Copy)
                    nc.scalar.activation(woT[:, :], banks[0][:, P:2 * P], ACT.Copy).then_inc(tw_out, 1)
                    act.wait_ge(vsum_ps, 1)
                    nc.scalar.activation(vsum[:, :], banks[1][:, 0:SEQS], ACT.Copy).then_inc(vsum_ready, 1)
            for s in range(SEQS):
                act.wait_ge(tx_ready, SEQS + s + 1)
                nc.scalar.activation(xtok[:, s * TPS:(s + 1) * TPS, :].rearrange("p n d -> p (n d)"), banks[s],
                                     ACT.Copy).then_inc(x0_ready, 1)

        @block.vector
        def _(dve):
            dve.sem_inc(qkn_ready, TWO)
            for released in (ss_ready, y_added, rot_parts, dif_ready, on_ready):
                dve.sem_inc(released, ONE)
            dve.wait_ge(vecs_in, 32)
            dve.wait_ge(consts_ready, 1)
            dve.wait_ge(zeros_ready, 13)

            def centre(n, s, src):
                dve.wait_ge(mean_ready, n + 1)
                nc.vector.tensor_tensor(fd[s][:, :], src, banks[s % 2], ALU.subtract).then_inc(fd_ready, 1)

            def ln_variance(n, s):
                dve.wait_ge(varp_ready, n + 1)
                nc.vector.tensor_scalar(var[:, s, :], banks[s % 2][:, 0:TPS], EPS, None, ALU.add).then_inc(var_ready, 1)

            def macaron_ln(n0):
                for pair in LN_PAIRS:
                    for s in pair:
                        centre(n0 + s, s, x0[:, s, :])
                    for s in pair:
                        ln_variance(n0 + s, s)
                    for s in pair:
                        dve.wait_ge(rb_ready, n0 + s + 1)
                        nc.vector.tensor_tensor(xa[:, s, 1:SP1], fd[s][:, :], banks[s % 2], ALU.mult).then_inc(xa_ready, 1)

            def split_qk_tile(TG):
                dve.wait_ge(xs_qk_hi_ready, TG + 1)
                nc.vector.tensor_tensor(xs_qk_lo[:, :], xs_qk[:, :], xs_qk_hi[:, :], ALU.subtract).then_inc(xs_qk_ready, 1)

            def split_v_tile(TG):
                dve.wait_ge(xs_v_hi_ready, TG + 1)
                nc.vector.tensor_tensor(xs_v_lo[:, :], xs_v[:, :], xs_v_hi[:, :], ALU.subtract).then_inc(xs_v_ready, 1)

            def rotate(U, t, h, sin):
                dve.wait_ge(sq_ready, U + 1)
                dve.wait_ge(rot_added, U - 1 + TWO)
                tt = t % TPS
                src = qk_ps[:, :, :].rearrange("p a (h d) -> p a h d", d=DH)
                tab = rot[:, :, :, :, :].rearrange("p t c a d -> p (t c a d)")

                def part(lo, n):
                    v = tab[:, bass.ds(tt * (4 * DH) + sin * 2 * DH, 2 * DH)].rearrange("p (a d) -> p a d", a=2)
                    return v[:, :, lo:lo + n].unsqueeze(2).to_broadcast([P, 2, UH, n])

                if not sin:
                    nc.vector.tensor_tensor(rot_c[h][:, :, :, :], src, part(0, DH), ALU.mult)
                else:
                    H2 = DH // 2
                    for lo in (0, H2):
                        to = H2 - lo
                        last = nc.vector.tensor_tensor(rot_s[h][:, :, :, to:to + H2], src[:, :, :, lo:lo + H2],
                                                       part(lo, H2), ALU.mult)
                    last.then_inc(rot_parts, 1)

            def square_sums(U, h):
                dve.wait_ge(halved, U + 1 + ONE)
                dve.wait_ge(rn_ready, U - 1 + TWO)
                nc.vector.tensor_reduce(ss[h][:, :], sq_half[:, :, :], AX_X, ALU.add).then_inc(ss_ready, 1)

            def rotary_share(U, h):
                dve.wait_ge(rot_parts, U + 1 + ONE)
                nc.vector.tensor_tensor(*(b[h][:, :, POOL_HEADS:UH, :] for b in (rot_sum, rot_c, rot_s)), ALU.add
                                        ).then_inc(rot_share, 1)

            def normalise(U, h):
                dve.wait_ge(rot_share, U + 1)
                dve.wait_ge(rot_added, U + 1 + TWO)
                dve.wait_ge(rn_ready, U + 1 + TWO)
                nc.vector.scalar_tensor_tensor(qkn[h][:, :, :, :].rearrange("p a h d -> p (a h) d"),
                                               rn[h][:, :].unsqueeze(2).to_broadcast([P, 2 * UH, DH]), NORM_LIMIT,
                                               rot_sum[h][:, :, :, :].rearrange("p a h d -> p (a h) d"), ALU.min, ALU.mult
                                               ).then_inc(qkn_ready, 1)

            def row_maxima(U, h):
                dve.wait_ge(s_ready, U + 1)
                nc.vector.tensor_reduce(row_max[h][:, :], s_ps[:, :].rearrange("p (a k) -> p a k", k=KEYS), AX_X, ALU.max
                                        ).then_inc(max_ready, 1)

            def differences(U, h):
                dve.wait_ge(max_ready, U + 1)
                nc.vector.tensor_tensor(dif[h][:, :, :], s_ps[:, :].rearrange("p (a k) -> p a k", k=KEYS),
                                        row_max[h][:, :].unsqueeze(2).to_broadcast([P, 2 * PAIRS, KEYS]), ALU.subtract
                                        ).then_inc(dif_ready, 1)

            def weighed():
                return o_ps[:, :, 0:PAIRS * DV].rearrange("p g (a d) -> p g a d", d=DV)

            def inverse_sums(U):
                dve.wait_ge(o_ready, U + 1 + TWO)
                nc.vector.reciprocal(rden[:, :, :].unsqueeze(3), weighed()[:, :, :, DH:DV]).then_inc(rden_ready, 1)

            def output_norm(U, h):
                dve.wait_ge(rden_ready, U + 1)
                nc.vector.tensor_tensor(on[h][:, :, :, :], weighed()[:, :, :, 0:DH],
                                        rden[:, :, :].unsqueeze(3).to_broadcast([P, 2, PAIRS, DH]), ALU.mult
                                        ).then_inc(on_ready, 1)

            def add_output(U, t, h):
                dve.wait_ge(y_ready, U + 1 + ONE)
                dve.wait_ge(y_added, U + ONE)
                at = (t // TPS) * SP1 + (t % TPS) * P + 1
                base = (xb if h else xa)[:, :, :].rearrange("p s n -> p (s n)")
                to = xb[:, :, :].rearrange("p s n -> p (s n)")
                nc.vector.tensor_tensor(to[:, bass.ds(at, P)], v_ps[:, 0:P], base[:, bass.ds(at, P)], ALU.add
                                        ).then_inc(y_added, 1)

            for p in range(2):
                if p == 0:
                    dve.wait_ge(x0_ready, SEQS)
                macaron_ln(first_ln(p))

                def parts(l, g):
                    def begin():
                        sc = scales[:, :, :, :].rearrange("p l a d -> p (l a d)")[:, bass.ds(l * (2 * DH), 2 * DH)]
                        nc.vector.tensor_tensor(rot[:, :, :, :, :].rearrange("p t c a d -> p (t c) (a d)"),
                                                rot_base[:, :, :, :].rearrange("p t a d -> p t (a d)"),
                                                sc.unsqueeze(1).to_broadcast([P, 2 * TPS, 2 * DH]), ALU.mult
                                                ).then_inc(rot_ready, 1)
                        split_qk_tile(g * TILES)
                        split_v_tile(g * TILES)
                        dve.wait_ge(rot_ready, g + 1)

                    def rotate_first(u):
                        if u == 1:
                            normalise(g * UNITS, 0)
                        rotate(g * UNITS + u, 0, u, False)
                        square_sums(g * UNITS + u, u)
                        rotate(g * UNITS + u, 0, u, True)
                        rotary_share(g * UNITS + u, u)

                    def ready():
                        dve.wait_ge(xa_ready, first_ln(p) + SEQS + SEQS * l)
                        NV = 3 + 2 * NCH
                        nc.vector.tensor_copy(vec[:, :], vecs[:, :, :].rearrange("p l v -> p (l v)")[:, bass.ds(l * NV, NV)]
                                              ).then_inc(vec_ready, 1)
                        split_qk_tile(g * TILES + 1)

                    def step(t, h, qk, v, mid, back1, back2):
                        U = g * UNITS + 2 * t + h
                        if v:
                            normalise(U + 1, 1 - h)
                        if qk:
                            rotate(U + 2, t + 1, h, False)
                            square_sums(U + 2, h)
                            rotate(U + 2, t + 1, h, True)
                        if mid:
                            row_maxima(U, h)
                        if qk:
                            rotary_share(U + 2, h)
                        if qk and h == 1 and tile_after_next(t):
                            split_qk_tile(g * TILES + t + 2)
                        if mid:
                            differences(U, h)
                        if back1:
                            inverse_sums(U - 1)
                        if v and h == 1:
                            split_v_tile(g * TILES + t + 1)
                        if back1:
                            output_norm(U - 1, 1 - h)
                        if back2:
                            add_output(U - 2, t - 1, h)

                    n0 = first_ln(p) + SEQS + SEQS * l

                    def mean(s):
                        centre(n0 + s, s, fs[s][:, :])

                    def variance(s):
                        ln_variance(n0 + s, s)

                    def spread(s):
                        dve.wait_ge(rb_ready, n0 + s + 1)
                        dve.wait_ge(fsq_ready, n0 + s + 1)
                        nc.vector.tensor_tensor(fd[s][:, :], fd[s][:, :], banks[s % 2], ALU.mult).then_inc(fn_raw, 1)
                        if s >= 2:
                            dve.wait_ge(gated_ps, g * SEQS * NCH + (s - 1) * NCH)
                        dve.wait_ge(fn_hi_ready, g * SEQS + s + 1)
                        nc.vector.tensor_tensor(fn_lo[s % 2][:, :], fn[s][:, :], fn_hi[s % 2][:, :].bitcast(F32), ALU.subtract).then_inc(fn_ready, 1)

                    def gated(s, j):
                        i, (c, m) = s * NCH + j, CHUNKS[j]
                        dve.wait_ge(gate_ready, g * SEQS * NCH + i + 1)
                        nc.vector.scalar_tensor_tensor(
                            hid[s % 2][j][0:m, :], banks[2 + 2 * (i % 2)][0:m, :], vec[0:m, 3 + j:4 + j], gate[i % 2][0:m, :],
                            ALU.add, ALU.mult).then_inc(hid_ready, 1)

                    def down(s):
                        dve.wait_ge(fy_ready, g * SEQS + s + 1 + ONE)
                        nc.vector.scalar_tensor_tensor(
                            xa[:, s, 1:SP1], banks[6 + s % 2], vec[:, 2:3], xb[:, s, 1:SP1], ALU.add, ALU.add
                        ).then_inc(xa_ready, 1)

                    return (begin, nothing, rotate_first, ready, step, nothing, mean, nothing, variance, spread, gated, down)

                over_layers(dve, p, parts)
                dve.wait_ge(xa_ready, first_ln(p) + SEQS + SEQS * DEPTH)
                for s in range(SEQS):
                    nc.vector.scalar_tensor_tensor(x0[:, s, :], xa[:, s, 1:SP1], 0.5, x0[:, s, :], ALU.mult, ALU.add
                                                   ).then_inc(x0_ready, 1)
                if p == 0:
                    dve.wait_ge(x0_ready, 2 * SEQS)
                    macaron_ln(first_ln(1) - SEQS)
                    dve.wait_ge(xa_ready, first_ln(1))
                    nc.vector.tensor_reduce(hsum[:, :], xa[:, :, 1:SP1], AX_X, ALU.add).then_inc(hsum_ready, 1)
                    dve.wait_ge(ymid_ps, 1)
                    nc.vector.tensor_tensor(x0[:, :, :], x0[:, :, :],
                                            banks[2][:, 0:SEQS].unsqueeze(2).to_broadcast([P, SEQS, SEQ]), ALU.add
                                            ).then_inc(x0_ready, SEQS)
                    dve.wait_ge(x0_ready, 3 * SEQS)

        @block.tensor
        def _(pe):
            for released in (y_ready, fy_ready):
                pe.sem_inc(released, ONE)
            pe.sem_inc(o_ready, TWO)
            pe.wait_ge(consts_in, 48)
            pe.wait_ge(x_in, 16)
            pe.wait_ge(mid_w_in, 32)
            for s in range(SEQS):
                for j in range(TPS):
                    last = nc.tensor.transpose(banks[s][:, j * P:(j + 1) * P], xtok[:, s * TPS + j, :], ident[:, :])
                last.then_inc(tx_ready, 1)

            def ln_mean(n, s, src):
                nc.tensor.matmul(banks[s % 2], mean_mat[:, :], src, start=True, stop=True).then_inc(mean_ready, 1)

            def ln_var(n, s):
                pe.wait_ge(fsq_ready, n + 1)
                for c in range(TPS):
                    last = nc.tensor.matmul(banks[s % 2][:, c:c + 1], fsq[s][:, c * P:(c + 1) * P],
                                            mean_mat[:, 0:1], start=True, stop=True)
                last.then_inc(varp_ready, 1)

            def ln_spread(n, s):
                pe.wait_ge(rstd_ready, n + 1)
                for c in range(TPS):
                    last = nc.tensor.matmul(banks[s % 2][:, c * P:(c + 1) * P],
                                            rstd[:, s, c:c + 1].to_broadcast([P, P]), ident[:, :], start=True, stop=True)
                last.then_inc(rb_ready, 1)

            def macaron_ln(n0):
                for pair in LN_PAIRS:
                    for s in pair:
                        if s >= 2:
                            pe.wait_ge(xa_ready, n0 + s - 1)
                        ln_mean(n0 + s, s, x0[:, s, :])
                    for s in pair:
                        ln_var(n0 + s, s)
                    for s in pair:
                        ln_spread(n0 + s, s)

            def project(hi, lo, h, part):
                dst = (qk_ps[:, 0, :], qk_ps[:, 1, :], v_ps[:, :])[part]
                cols = slice(part * INNER + h * HALF, part * INNER + (h + 1) * HALF)
                nc.tensor.matmul(dst, hi[:, :], wqkv_hi[:, cols], start=True, stop=False)
                nc.tensor.matmul(dst, hi[:, :], wqkv_lo[:, cols], start=False, stop=False)
                return nc.tensor.matmul(dst, lo[:, :], wqkv_hi[:, cols], start=False, stop=True)

            def project_qk(U, TG, h):
                pe.wait_ge(xs_qk_ready, TG + 1)
                pe.wait_ge(rot_parts, U + ONE)
                project(xs_qk_hi, xs_qk_lo, h, 0)
                project(xs_qk_hi, xs_qk_lo, h, 1).then_inc(qk_ready, 1)

            def project_v(U, TG, h, Y):
                pe.wait_ge(xs_v_ready, TG + 1)
                pe.wait_ge(vn_ready, U + ONE)
                if Y is not None:
                    pe.wait_ge(y_added, Y + 1 + ONE)
                project(xs_v_hi, xs_v_lo, h, 2).then_inc(v_ready, 1)

            def heads_major(U, t, h):
                pe.wait_ge(qkn_ready, U + 1 + TWO)
                pe.wait_ge(qbd_ready, U + ONE)
                if not (isinstance(t, int) and t == 0):
                    pe.wait_ge(pt_ready, U - 1)
                for a in range(PAIRS):
                    last = nc.tensor.transpose(tr0[:, a * P:(a + 1) * P],
                                               qkn[h][:, 0, 2 * a:2 * a + 2, :].rearrange("p h d -> p (h d)"), ident[:, :])
                last.then_inc(qt_ready, 1)
                pe.wait_ge(kt_ready, U + ONE)
                if not (isinstance(t, int) and t == 0):
                    pe.wait_ge(ot_ready, U - 2 + ONE)
                for a in range(PAIRS):
                    last = nc.tensor.transpose(tr1[:, a * P:(a + 1) * P],
                                               qkn[h][:, 1, 2 * a:2 * a + 2, :].rearrange("p h d -> p (h d)"), ident[:, :])
                last.then_inc(ktp_ready, 1)

            def scores(U, t, h):
                pe.wait_ge(qbd_ready, U + 1 + ONE)
                pe.wait_ge(kt_ready, U + 1 + ONE)
                pe.wait_ge(dif_ready, U + ONE)
                pe.wait_ge(consts_ready, 1)
                m = mask[:, :, :].rearrange("p t k -> p (t k)")[:, bass.ds(t * (2 * KEYS), 2 * KEYS)]
                nc.tensor.matmul(s_ps[:, :], ident16[:, :], m.unsqueeze(1).to_broadcast([P, PAIRS, 2 * KEYS]),
                                 start=True, stop=False, skip_group_check=True)
                for a in range(PAIRS):
                    for gg in range(2):
                        for ws in range(2):
                            w = 2 * gg + ws
                            last = nc.tensor.matmul(
                                s_ps[ws * 64:(ws + 1) * 64, (2 * a + gg) * KEYS:(2 * a + gg + 1) * KEYS],
                                qbd[h][:, a, w, :, :].rearrange("p b q -> p (b q)"),
                                kt[h][:, a, w * WIN:w * WIN + KEYS], start=False, stop=True, skip_group_check=True)
                last.then_inc(s_ready, 1)

            def prob_major(U, h, mid):
                pe.wait_ge(prob_ready, U + 1)
                if mid:
                    pe.wait_ge(qbd_ready, U + 2 + ONE)
                else:
                    pe.wait_ge(pt_ready, U)
                for a in range(PAIRS):
                    last = nc.tensor.transpose(tr0[:, a * P:(a + 1) * P],
                                               prob[h][:, 2 * a:2 * a + 2, :].rearrange("p g k -> p (g k)"), ident[:, :])
                last.then_inc(ptp_ready, 1)

            def out_major(U, h, mid):
                pe.wait_ge(on_ready, U + 1 + ONE)
                if mid:
                    pe.wait_ge(kt_ready, U + 3 + ONE)
                else:
                    pe.wait_ge(ot_ready, U + ONE)
                for gg in range(2):
                    for pg in range(PAIRS // 2):
                        c = gg * (PAIRS // 2) + pg
                        last = nc.tensor.transpose(tr1[:, c * P:(c + 1) * P],
                                                   on[h][:, gg, 2 * pg:2 * pg + 2, :].rearrange("p a d -> p (a d)"),
                                                   ident[:, :])
                last.then_inc(otp_ready, 1)

            def wait_to_weigh(U, TG, h):
                pe.wait_ge(pt_ready, U + 1)
                pe.wait_ge(vs_in[h], TG * 16 + 16 + DMA_ONE)
                pe.wait_ge(vhead_in[h], TG * 16 + 16)
                pe.wait_ge(on_ready, U + ONE)

            def weigh_values(h):
                for gg in range(2):
                    rows = slice(gg * KEYS, (gg + 1) * KEYS)
                    for a in range(PAIRS):
                        for ws in range(2):
                            for hp in range(2):
                                c = 2 * ws + hp
                                last = nc.tensor.matmul(
                                    o_ps[c * WIN:(c + 1) * WIN, gg, a * DV:(a + 1) * DV],
                                    pt[h][rows, a, c * WIN:(c + 1) * WIN],
                                    (vn if ws else vs)[h][rows, 2 * a + hp, :],
                                    start=True, stop=True, skip_group_check=True)
                last.then_inc(o_ready, 1)

            def project_out(U, h, last_v):
                pe.wait_ge(ot_ready, U + 1 + ONE)
                pe.wait_ge(vn_ready, last_v + ONE)
                pe.wait_ge(y_added, U + ONE)
                n = 0
                for pg in range(PAIRS // 2):
                    for hp in range(2):
                        last = nc.tensor.matmul(v_ps[:, 0:P], wo[:, h, pg, hp, :], ot[h][:, :, pg, :, hp, :],
                                                start=n == 0, stop=n == PAIRS - 1)
                        n += 1
                last.then_inc(y_ready, 1)

            for p in range(2):
                pe.wait_ge(x0_ready, SEQS if p == 0 else 3 * SEQS)
                pe.wait_ge(zeros_ready, 13)
                macaron_ln(first_ln(p))

                def parts(l, g):
                    def project_first(u):
                        if u == 0:
                            pe.wait_ge(wqkv_split, g + 1 + ONE)
                            if isinstance(l, int):
                                pe.wait_ge(xa_ready, first_ln(p) + SEQS)
                            else:
                                pe.wait_ge(fn_raw, g * SEQS)
                        project_qk(g * UNITS + u, g * TILES, u)

                    def ready():
                        pe.wait_ge(xa_ready, first_ln(p) + SEQS + SEQS * l)
                        pe.wait_ge(wo_in, 16 * g + 16)

                    def step(t, h, qk, v, mid, back1, back2):
                        U = g * UNITS + 2 * t + h
                        if mid:
                            heads_major(U, t, h)
                        if qk:
                            project_qk(U + 2, g * TILES + t + 1, h)
                        if mid:
                            project_v(U, g * TILES + t, h, U - 3 if back2 else None)
                        if back1:
                            prob_major(U - 1, 1 - h, mid)
                        if back1 and not back2:
                            wait_to_weigh(U - 1, g * TILES + t - 1 + h, 1 - h)
                        if mid:
                            scores(U, t, h)
                        if back1 and back2:
                            wait_to_weigh(U - 1, g * TILES + t - 1 + h, 1 - h)
                        if back2:
                            out_major(U - 2, h, mid)
                        if back1:
                            weigh_values(1 - h)
                        if back2:
                            project_out(U - 2, h, U + 1 if mid else (g + 1) * UNITS)

                    n0 = first_ln(p) + SEQS + SEQS * l

                    def mean(s):
                        pe.wait_ge(fs_ready, g * SEQS + s + 1)
                        if s == 0:
                            pe.wait_ge(rot_parts, g * UNITS + UNITS + ONE)
                        if s >= 2:
                            pe.wait_ge(fn_raw, g * SEQS + s - 1)
                        ln_mean(n0 + s, s, fs[s][:, :])

                    def variance(s):
                        ln_var(n0 + s, s)

                    def spread(s):
                        ln_spread(n0 + s, s)

                    def gated(s, j):
                        i, (c, m) = s * NCH + j, CHUNKS[j]
                        if i == 0:
                            pe.wait_ge(w1_split, g + 1 + ONE)
                            pe.wait_ge(y_added, g * UNITS + UNITS + ONE)
                        if j == 0:
                            pe.wait_ge(fn_ready, g * SEQS + s + 1)
                        if i >= 2:
                            pe.wait_ge(hid_ready, g * SEQS * NCH + i - 1)
                        for part in range(2):
                            dst = banks[2 + 2 * (i % 2) + part][0:m, :]
                            cols = slice(part * HID + c, part * HID + c + m)
                            nc.tensor.matmul(dst, w1_hi[:, cols], fn_hi[s % 2][:, :], start=True, stop=False)
                            nc.tensor.matmul(dst, w1_hi[:, cols], fn_lo[s % 2][:, :], start=False, stop=False)
                            last = nc.tensor.matmul(dst, w1_lo[:, cols], fn_hi[s % 2][:, :], start=False, stop=True)
                        last.then_inc(gated_ps, 1)

                    def down(s):
                        if s == 0:
                            pe.wait_ge(w2_in, 16 * NCH * g + 16 * NCH)
                        if s >= 2:
                            pe.wait_ge(xa_ready, n0 + s - 1)
                        for j, (c, m) in enumerate(CHUNKS):
                            pe.wait_ge(hid_ready, g * SEQS * NCH + s * NCH + j + 1)
                            last = nc.tensor.matmul(banks[6 + s % 2], w2[0:m, j, :], hid[s % 2][j][0:m, :],
                                                    start=j == 0, stop=j == NCH - 1)
                        last.then_inc(fy_ready, 1)

                    return (nothing, project_first, nothing, ready, step, nothing, mean, nothing, variance, spread, gated, down)

                over_layers(pe, p, parts)
                pe.wait_ge(x0_ready, 2 * SEQS if p == 0 else 4 * SEQS)
                if p == 0:
                    macaron_ln(first_ln(1) - SEQS)
                    pe.wait_ge(xa_ready, first_ln(1))
                    nc.tensor.transpose(banks[0][:, 0:P], wqkv_rows[:, :], ident[:, :])
                    nc.tensor.transpose(banks[0][:, P:2 * P], wo_rows[:, :], ident[:, :]).then_inc(tw_ready, 1)
                    pe.wait_ge(tw_out, 1)
                    pe.wait_ge(hsum_ready, 1)
                    nc.tensor.matmul(banks[1][:, 0:SEQS], wvT[:, :], hsum[:, :], start=True, stop=True).then_inc(vsum_ps, 1)
                    pe.wait_ge(vsum_ready, 1)
                    nc.tensor.matmul(banks[2][:, 0:SEQS], woT[:, :], vsum[:, :], start=True, stop=True).then_inc(ymid_ps, 1)
            for s in range(SEQS):
                for j in range(TPS):
                    last = nc.tensor.transpose(banks[s][:, j * P:(j + 1) * P], x0[:, s, j * P:(j + 1) * P], ident[:, :])
                last.then_inc(tx_ready, 1)


def layer_vectors(ln_g, ln_b, b1, b2):
    out = np.zeros((P, DEPTH, 3 + 2 * NCH), np.float32)
    for i, v in enumerate((ln_g, ln_b, b2)):
        out[:, :, i] = v.T
    for part in range(2):
        for j, (c, n) in enumerate(CHUNKS):
            out[0:n, :, 3 + part * NCH + j] = b1[:, part * HID + c:part * HID + c + n].T
    return out


def wo_rows_by_pair(w):
    return w.reshape(DEPTH, HEADS // 4, 2, 2, DH, P).transpose(0, 2, 4, 1, 3, 5).reshape(DEPTH, P, -1)


def kernel(**inputs):
    import ml_dtypes
    from concourse import bacc
    from concourse.bass_utils import run_bass_kernel_spmd

    given = {name.removeprefix("L0_"): np.asarray(a) for name, a in inputs.items()}
    x = given["attn_x"]
    nc = bacc.Bacc("TRN2", target_bir_lowering=False, num_devices=1)
    arrays = {
        "x_dram": x.reshape(-1, P),
        "w_qkv_dram": given["attn_w_qkv"],
        "w_o_dram": given["attn_w_o"],
        "layer_wqkv_dram": given["ffn_Wqkv"],
        "layer_wo_dram": wo_rows_by_pair(given["ffn_Wo"]),
        "layer_w1_dram": given["ffn_W1"],
        "layer_w2_dram": given["ffn_W2"],
        "layer_scales_dram": np.stack([given["ffn_q_scale"], given["ffn_k_scale"]], 1),
        "layer_vectors_dram": layer_vectors(*(given["ffn_" + n] for n in ("ln_g", "ln_b", "b1", "b2"))),
        "rotary_base_dram": rotary_base().reshape(P, TPS * 2, 2, DH),
        "score_mask_dram": score_mask().astype(ml_dtypes.bfloat16),
        "identity_dram": np.eye(P, dtype=np.float32),
    }
    arrays = {name: np.ascontiguousarray(a) for name, a in arrays.items()}
    args = [nc.dram_tensor(name, a.shape, mybir.dt.from_np(a.dtype), kind="ExternalInput").ap()
            for name, a in arrays.items()]
    out = nc.dram_tensor("out", (SEQS * SEQ, P), F32, kind="ExternalOutput").ap()
    build(nc, *args, out)
    r = run_bass_kernel_spmd(nc, [arrays], core_ids=[0])
    return r.results[0]["out"].reshape(x.shape)
```
